# Optimizing a Trainium2 kernel written in Bass

```python
import numpy as np
import jax
import jax.numpy as jnp

def _softmax(x, axis=-1):
    return jax.nn.softmax(x, axis=axis)

def _gelu(x):
    return jax.nn.gelu(x, approximate=True)

def _silu(x):
    return jax.nn.silu(x)

def _sigmoid(x):
    return jax.nn.sigmoid(x)

def _layernorm(x, axis=-1, eps=1e-05):
    m = jnp.mean(x, axis=axis, keepdims=True)
    v = jnp.var(x, axis=axis, keepdims=True)
    return (x - m) / jnp.sqrt(v + eps)

def _scatter_add(tgt, idx, src, axis=0):
    return tgt.at[idx].add(src)

def _segment_sum(src, seg, n):
    return jax.ops.segment_sum(src, seg, n)
kernel_name = 'mk_xattn_ffn_d1_seqx_r2_80f759'

def setup_inputs(seed: int=0):
    np.random.seed(seed)
    _w = jnp.asarray

    def _rec_inputs():
        import jax
        import jax.numpy as jnp
        _rk = jax.random.key(seed)
        x = -0.000125 + 0.9999 * jax.random.normal(jax.random.fold_in(_rk, 1), (8, 100, 512), jnp.float32)
        _lenS = 100 - jax.random.randint(jax.random.fold_in(_rk, 7), (8,), 0, max(1, 100 // 4) + 1, jnp.int32)
        _lenS2 = 722 - jax.random.randint(jax.random.fold_in(_rk, 8), (8,), 0, max(1, 722 // 4) + 1, jnp.int32)
        _ctx_1024P = jax.random.normal(jax.random.fold_in(_rk, 11), (8, 16, 512), jnp.float32)
        _ctx_1024c = jax.random.dirichlet(jax.random.fold_in(_rk, 511), 0.3 * jnp.ones((16,), jnp.float32), (8, 722))
        _ctx_1024t = jnp.einsum('bsk,bkd->bsd', _ctx_1024c, _ctx_1024P)
        _ctx_1024t = _ctx_1024t * jax.lax.rsqrt(jnp.mean(jnp.square(_ctx_1024t)) + 1e-12) * 0.953939
        ctx_1024 = -1.78809e-06 + 0.0312453 * (_ctx_1024t + 0.3 * jax.random.normal(jax.random.fold_in(_rk, 611), (8, 722, 512), jnp.float32))
        return (x, ctx_1024)
    x, ctx_1024 = _rec_inputs()

    def _L0_xattn_setup():
        import jax, jax.numpy as jnp
        import numpy as np
        E, T, H, F = (16, 1024, 512, 2048)
        key = jax.random.key(seed)
        kx, k1, k2, k3 = jax.random.split(key, 4)
        s = 1.0 / np.sqrt(H)
        return {'x': jax.random.normal(kx, (E, T, H), dtype=jnp.float32), 'w1': jax.random.normal(k1, (E, F, H), dtype=jnp.float32) * s, 'v1': jax.random.normal(k2, (E, F, H), dtype=jnp.float32) * s, 'w2': jax.random.normal(k3, (E, F, H), dtype=jnp.float32) * s}
    _L0_xattn_all = _L0_xattn_setup()
    _L0_xattn_in = {k: v for k, v in _L0_xattn_all.items() if k in ()}
    del _L0_xattn_all

    def _L0_ffn_setup():
        import jax, jax.numpy as jnp
        import numpy as np
        B, S, D, F, E = (2, 1024, 512, 1024, 16)
        key = jax.random.key(seed)
        k = jax.random.split(key, 4)
        scale1 = float(np.sqrt(2.0 / D))
        scale2 = float(np.sqrt(2.0 / F))
        return {'h': jax.random.normal(k[0], (B, S, D), dtype=jnp.float32), 'router_w': jax.random.normal(k[1], (D, E), dtype=jnp.float32) * (1.0 / np.sqrt(D)), 'w1': jax.random.normal(k[2], (E, D, F), dtype=jnp.float32) * scale1, 'b1': jnp.zeros((E, F), dtype=jnp.float32), 'w2': jax.random.normal(k[3], (E, F, D), dtype=jnp.float32) * scale2, 'b2': jnp.zeros((E, D), dtype=jnp.float32)}
    _L0_ffn_all = _L0_ffn_setup()
    _L0_ffn_in = {k: v for k, v in _L0_ffn_all.items() if k in ('router_w', 'w1', 'b1', 'w2', 'b2')}
    del _L0_ffn_all
    return {'x': x, 'ctx_1024': ctx_1024, 'L0_ffn_router_w': _L0_ffn_in['router_w'], 'L0_ffn_w1': _L0_ffn_in['w1'], 'L0_ffn_b1': _L0_ffn_in['b1'], 'L0_ffn_w2': _L0_ffn_in['w2'], 'L0_ffn_b2': _L0_ffn_in['b2']}

def reference(x, ctx_1024, L0_ffn_router_w, L0_ffn_w1, L0_ffn_b1, L0_ffn_w2, L0_ffn_b2):
    import jax
    import jax.numpy as jnp

    def _L0_xattn_ref(x, w1, v1, w2):
        import jax, jax.numpy as jnp
        import numpy as np
        E, T, H, F = (16, 1024, 512, 2048)
        x1 = jnp.einsum('eth,efh->etf', x, w1)
        x2 = jnp.einsum('eth,efh->etf', x, v1)
        h = jax.nn.gelu(x1, approximate=True) * x2
        return jnp.einsum('etf,efh->eth', h, w2)

    def _L0_ffn_ref(h, router_w, w1, b1, w2, b2):
        import jax, jax.numpy as jnp
        import numpy as np
        B, S, D, F, E = (2, 1024, 512, 1024, 16)
        b, s, d = h.shape
        x = h.reshape(-1, d)
        logits = x @ router_w
        assign = jnp.argmax(logits, axis=-1)
        w = jax.nn.sigmoid(jnp.take_along_axis(logits, assign[:, None], axis=1)[:, 0])
        hh = jnp.einsum('nd,edf->nef', x, w1) + b1
        hh = jax.nn.gelu(hh, approximate=False)
        all_out = jnp.einsum('nef,efd->ned', hh, w2) + b2
        out = jnp.take_along_axis(all_out, assign[:, None, None], axis=1)[:, 0, :]
        out = out * w[:, None]
        return out.reshape(b, s, d)
    x = x + _L0_xattn_ref(_layernorm(x, axis=-1), ctx_1024, ctx_1024, ctx_1024)
    x = x + _L0_ffn_ref(_layernorm(x, axis=-1), L0_ffn_router_w, L0_ffn_w1, L0_ffn_b1, L0_ffn_w2, L0_ffn_b2)
    return x

_drawn_inputs = setup_inputs


def setup_inputs(seed=0):
    import zlib

    import numpy as np

    out = dict(_drawn_inputs(seed))
    spreads = {'L0_ffn_b1': (0.0, 0.416), 'L0_ffn_b2': (0.0, 0.407)}
    factors = {}
    for name, (base, spread) in spreads.items():
        noise = np.random.default_rng([zlib.crc32(name.encode()), seed]).standard_normal(out[name].shape)
        drawn = base * np.exp(spread * noise) if base else spread * noise
        out[name] = jnp.asarray(drawn.astype(out[name].dtype))
    for name, factor in factors.items():
        out[name] = (out[name] * factor).astype(out[name].dtype)
    return out
```

```python
from contextlib import ExitStack
from itertools import chain

import numpy as np

import concourse.bass as bass
from concourse import mybir

F32 = mybir.dt.float32
I32 = mybir.dt.int32
U32 = mybir.dt.uint32
ALU = mybir.AluOpType
ACT = mybir.ActivationFunctionType
AX = mybir.AxisListType

P = 128
NB, T, D, S = 8, 100, 512, 722
E, F = 16, 1024
TOK = NB * T
KD = D // P
KF = F // P
SC = -(-S // P)
CW = [min(P, S - P * c) for c in range(SC)]
SA = 3 * P
BLK = 64
MAXB = E - 1 + -(-(TOK - E + 1) // BLK)
NCOL = MAXB + 2
NTHR = TOK // BLK
SLOTS = 3
RING = 3
HD = D // 2
XW = HD + 1
EPS = 1e-5

C_ID, C_ONE = 0, P
C_TRI = C_ONE + P
C_EM = C_TRI + T
C_THR = C_EM + E
C_PM = C_THR + NTHR
C_BLK = C_PM + BLK
C_TOK = C_BLK + NCOL
C_LT = C_TOK + NB
C_E = C_LT + E * E
C_HALF = C_E + E
C_NH = C_HALF + 1
C_ALL = C_NH + 1


def shape_constants():
    c = np.zeros((P, C_ALL), np.float32)
    p = np.arange(P)
    c[:, C_ID:C_ID + P] = np.eye(P)
    c[:, C_ONE:C_ONE + P] = 1
    c[:, C_TRI:C_TRI + T] = p[:, None] < np.arange(T)
    c[:, C_EM:C_EM + E] = np.arange(E) - E
    c[:, C_THR:C_THR + NTHR] = BLK * (1 + np.arange(NTHR))
    c[:, C_PM:C_PM + BLK] = np.arange(BLK)
    c[:, C_BLK:C_BLK + NCOL] = np.arange(NCOL)
    c[:, C_TOK:C_TOK + NB] = p[:, None] + T * np.arange(NB) - TOK
    c[:, C_LT:C_LT + E * E] = (np.arange(E)[:, None] > np.arange(E)).ravel()
    c[:, C_E:C_E + E] = np.arange(E)
    c[:, C_HALF] = 2 * TOK + p // BLK
    c[:, C_NH] = -0.5
    return c


def build(nc, x, ctx_main, ctx_rest, router, w1, b1, w2, b2, consts, out):
    t_rows = nc.dram_tensor("t_rows", (TOK, D), F32).ap()
    xw_rows = nc.dram_tensor("xw_rows", (2 * TOK, XW), F32).ap()
    xw_by_token = xw_rows.rearrange("(n h) d -> n h d", h=2)
    out_halves = out.rearrange("b t (h d) -> (b t h) d", h=2)

    with ExitStack() as stack:
        def sb(name, shape, dt=F32):
            return stack.enter_context(nc.sbuf_tensor(name, shape, dt))

        def sem(name):
            return stack.enter_context(nc.semaphore(name))

        def sems(name, n):
            return [sem(f"{name}{i}") for i in range(n)]

        W1 = sb("W1", [P, SLOTS, KD, F])
        W2 = sb("W2", [P, SLOTS, KF, D])
        con = sb("con", [P, C_ALL])
        rw = sb("rw", [P, KD, E])
        b1s = sb("b1s", [P, E, KF])
        xin = sb("xin", [T, RING, D])
        work = sb("work", [P, RING * SC * D])
        ctxT = sb("ctxT", [P, KD, S])
        xn = sb("xn", [T, D])
        xnT = sb("xnT", [P, KD, T])
        hid = sb("hid", [T, S])
        hidT = sb("hidT", [P, SC, T])
        xw = sb("xw", [T, RING, 2, XW])
        tn = sb("tn", [T, D])
        tT = sb("tT", [P, KD, T])
        bn_x, ag_x, ve_x, rs_x = sb("bn_x", [T, 6]), sb("ag_x", [T, 2]), sb("ve_x", [T, 1]), sb("rs_x", [T, 1])
        bn_t, ag_t, ve_t, rs_t = sb("bn_t", [T, 6]), sb("ag_t", [T, 2]), sb("ve_t", [T, 1]), sb("rs_t", [T, 1])
        top, cand, who, gate = sb("top", [T, 1]), sb("cand", [T, E]), sb("who", [T, 1]), sb("gate", [T, 1])
        hot, hot_sum, hot_all = sb("hot", [T, E]), sb("hot_sum", [T, E]), sb("hot_all", [T, NB, E])
        rank_tmp, rank, over = sb("rank_tmp", [T, E]), sb("rank", [T, 1]), sb("over", [T, NTHR])
        quot, quot_all, rest = sb("quot", [T, 1]), sb("quot_all", [T, NB]), sb("rest", [T, 1])
        row_hot = sb("row_hot", [T, NB, BLK])
        cnt_over = ctxT[:, 0, 0:E * NTHR].rearrange("p (e n) -> p e n", e=E)
        before = ctxT[:, 1, 0:E * E].rearrange("p (e n) -> p e n", e=E)
        start_tok = ctxT[0:T, 2, 0:NB * E].rearrange("p (b e) -> p b e", b=NB)
        blk_hot = ctxT[0:T, 3, 0:NB * NCOL].rearrange("p (b n) -> p b n", b=NB)
        extra, start, blk_of = sb("extra", [P, E]), sb("start", [P, E]), sb("blk_of", [T, NB])
        ends = sb("ends", [P, E + 1], I32)
        id_tok, id_half = sb("id_tok", [P, NCOL], U32), sb("id_half", [P, NCOL], U32)
        at_t, at_x, at_out = ([sb(f"{n}{i}", [P, 1], U32) for i in range(2)] for n in ("at_t", "at_x", "at_out"))

        cxs = [work[:, SC * D * i:SC * D * (i + 1)].rearrange("p (c d) -> p c d", c=SC) for i in range(RING)]
        used = [0]

        def part2(n):
            used[0] += n
            assert used[0] <= RING * SC * D
            return work[:, used[0] - n:used[0]]
        g_t = [part2(D) for _ in range(2)]
        g_x2 = part2(2 * XW)
        g_x = [g_x2[:, XW * i:XW * i + XW] for i in range(2)]
        blkT = part2(KD * BLK).rearrange("p (k t) -> p k t", k=KD)
        h_pre = part2(D)
        hT = part2(KF * BLK).rearrange("p (c t) -> p c t", c=KF)
        y_b = part2(HD)
        y_out2 = part2(2 * HD)
        y_out = [y_out2[:, HD * i:HD * i + HD] for i in range(2)]
        b2s = part2(SLOTS * HD).rearrange("p (s d) -> p s d", s=SLOTS)

        ident, ones = con[:, C_ID:C_ID + P], con[:, C_ONE:C_ONE + P]
        tri, e_low = con[0:T, C_TRI:C_TRI + T], con[0:T, C_EM:C_EM + E]
        thr = con[:, C_THR:C_THR + NTHR]
        rows64, blks = con[0:T, C_PM:C_PM + BLK], con[0:T, C_BLK:C_BLK + NCOL]
        tok_low = con[0:T, C_TOK:C_TOK + NB]
        e_before = con[:, C_LT:C_LT + E * E].rearrange("p (e n) -> p e n", e=E)
        e_num, halves, neg_half = con[:, C_E:C_E + E], con[:, C_HALF:C_HALF + 1], con[0:T, C_NH:C_NH + 1]

        bank = [stack.enter_context(nc.psum_tensor(f"bank{i}", [P, 512], F32)) for i in range(8)]
        p_xa, p_xb, p_t, p_att, p_lg = bank[0], bank[1], bank[2], bank[6], bank[7]
        p_rk = p_lg[:, 64:128]
        p_c = bank[3:6]
        p_h, p_hT, p_blk, p_y = bank[0], bank[1], bank[2], bank[5]

        s_con, s_out0 = sem("s_con"), sem("s_out0")
        s_x, s_ctx = sems("s_x_in", RING), sems("s_ctx", RING)
        s_w1, s_w2, s_b2 = sems("s_w1", SLOTS), sems("s_w2", SLOTS), sems("s_b2", SLOTS)
        s_trow, s_xwrow = sem("s_trow"), sems("s_xwrow", RING)
        s_x1ps, s_tps, s_cps, s_lgps = sem("s_x1ps"), sem("s_tps"), sem("s_cps"), sem("s_lgps")
        s_hps, s_xnps, s_att, s_rkps = sem("s_hps"), sem("s_xnps"), sem("s_att"), sem("s_rkps")
        s_cntps, s_idps = sem("s_cntps"), sem("s_idps")
        s_gelu, s_tT, s_ctxA, s_hidT = sem("s_gelu"), sem("s_tT"), sem("s_ctxA"), sem("s_hidT")
        s_tanh, s_xnT = sem("s_tanh"), sem("s_xnT")
        s_ctxD = sem("s_ctxD")
        s_bnx, s_agx, s_vex, s_rsx, s_xn = (sem(n) for n in ("s_bnx", "s_agx", "s_vex", "s_rsx", "s_xn"))
        s_bnt, s_agt, s_vet, s_rst, s_t = (sem(n) for n in ("s_bnt", "s_agt", "s_vet", "s_rst", "s_t"))
        s_hid, s_x2, s_top, s_cand, s_who, s_hot = (
            sem(n) for n in ("s_hid", "s_x2", "s_top", "s_cand", "s_who", "s_hot"))
        s_sum, s_rank, s_over, s_quot, s_rest, s_rowhot, s_gate = (
            sem(n) for n in ("s_sum", "s_rank", "s_over", "s_quot", "s_rest", "s_rowhot", "s_gate"))
        s_table, s_blkhot, s_ids, s_g0 = sem("s_table"), sem("s_blkhot"), sem("s_ids"), sem("s_g0")
        s_table2, s_yb_used, s_y_free = sem("s_table2"), sem("s_yb_used"), sem("s_y_free")
        s_apart_v, s_apart_p = sem("s_apart_v"), sem("s_apart_p")
        s_bps, s_hp, s_hTp, s_y = sem("s_bps"), sem("s_hp"), sem("s_hTp"), sem("s_y")
        s_w1_used, s_w2_used = sem("s_w1_used"), sem("s_w2_used")
        s_blkT, s_act = sem("s_blkT"), sem("s_act")
        s_hc, s_hb, s_yb, s_yo = sem("s_hc"), sem("s_hb"), sem("s_yb"), sem("s_yo")
        s_at_t, s_at_x, s_at_out = sem("s_at_t"), sem("s_at_x"), sem("s_at_out")
        s_gt, s_gx, s_done = sems("s_gt", 2), sem("s_gx"), sem("s_done")

        block = stack.enter_context(nc.Block())

        def batches(eng, step):
            step(0, 0, 0, True, False)
            with eng.Fori(0, (NB - 2) // RING) as i:
                for u in range(RING):
                    step(RING * i + (1 + u), i + (1 + u) // RING, (1 + u) % RING, False, False)
            step(NB - 1, (NB - 1) // RING, (NB - 1) % RING, False, True)

        def last_block(eng):
            return eng.value_load(ends[0:1, E:E + 1], min_val=E - 1, max_val=MAXB - 1)

        def blocks_of_experts(eng, unit):
            def rest_of(e, rnd, slot, first, end):
                with eng.If(end > first + 1):
                    with eng.Fori(first + 1, end) as j:
                        unit(j, e, rnd, slot, slot, False)

            def expert(e, rnd, slot):
                first = eng.value_load(ends[0:1, bass.ds(e - 1, 1)], min_val=1, max_val=MAXB - 1)
                end = eng.value_load(ends[0:1, bass.ds(e, 1)], min_val=2, max_val=MAXB)
                unit(first, e, rnd, slot, (slot - 1) % SLOTS, True)
                rest_of(e, rnd, slot, first, end)

            end = eng.value_load(ends[0:1, 0:1], min_val=1, max_val=MAXB - E + 1)
            unit(0, 0, 0, 0, None, True)
            rest_of(0, 0, 0, 0, end)
            with eng.Fori(0, (E - 1) // SLOTS) as g:
                for s in range(SLOTS):
                    expert(SLOTS * g + (1 + s), g + (1 + s) // SLOTS, (1 + s) % SLOTS)
            assert (E - 1) % SLOTS == 0
            return last_block(eng)

        @block.sync
        def _(sp):
            def load_batch(b):
                r = b % RING
                sp.dma_start(xin[:, r, :], x[b]).then_inc(s_x[r], 16)
                sp.dma_start(cxs[r][:, 0:SC - 1, :], ctx_main[b]).then_inc(s_ctx[r], 16)
                sp.dma_start(cxs[r][0:CW[-1], SC - 1, :], ctx_rest[b]).then_inc(s_ctx[r], 16)

            def load_half(dst, src, signal):
                n = dst.shape[1] // 2
                for h in range(2):
                    sp.dma_start(dst[:, n * h:n * h + n], src[:, n * h:n * h + n]).then_inc(signal, 16)

            load_batch(0)
            sp.dma_start(con[:, :], consts).then_inc(s_con, 16)
            sp.dma_start(rw[:, :, :], router).then_inc(s_con, 16)
            sp.dma_start(b1s[:, :, :], b1).then_inc(s_con, 16)
            load_batch(1)
            load_batch(2)
            for b in range(NB):
                if b // 2 < SLOTS:
                    W, w, signal = (W1, w1, s_w1) if b % 2 == 0 else (W2, w2, s_w2)
                    load_half(W[:, b // 2], w[b // 2], signal[b // 2])
                sp.wait_ge(s_t, b + 1)
                sp.dma_start(t_rows[T * b:T * b + T, :], tn[:, :]).then_inc(s_trow, 16)
                if b + RING < NB:
                    sp.wait_ge(s_att, b + 1)
                    sp.wait_ge(s_x2, b + 1)
                    load_batch(b + RING)
                sp.wait_ge(s_gate, b + 1)
                sp.dma_start(xw_by_token[T * b:T * b + T], xw[:, b % RING]).then_inc(s_xwrow[b % RING], 16)
            sp.wait_ge(s_att, NB)
            for s in range(SLOTS):
                for h in range(2):
                    sp.dma_start(b2s[BLK * h:BLK * h + BLK, s], b2[s, h].partition_broadcast(BLK)
                                 ).then_inc(s_b2[s], 16)

            def load_expert(e, rnd, s):
                one = bass.ds(e, 1)
                sp.wait_ge(s_w1_used, e - 1)
                load_half(W1[:, s], w1[one].rearrange("o p k f -> (o p) k f"), s_w1[s])
                sp.wait_ge(s_w2_used, e - 2)
                load_half(W2[:, s], w2[one].rearrange("o p k f -> (o p) k f"), s_w2[s])
                sp.wait_ge(s_yb_used, e - 2)
                for h in range(2):
                    sp.dma_start(b2s[BLK * h:BLK * h + BLK, s], b2[one, h].partition_broadcast(BLK)
                                 ).then_inc(s_b2[s], 16)

            with sp.Fori(1, E // SLOTS) as g:
                for s in range(SLOTS):
                    load_expert(SLOTS * g + s, g, s)
            load_expert(E - 1, E // SLOTS, 0)

        @block.tensor
        def _(pe):
            def context_transposes(place, c):
                for k in range(KD):
                    last = nc.tensor.transpose(p_c[c % 3][:, P * k:P * k + CW[c]],
                                               cxs[place][0:CW[c], c, P * k:P * k + P],
                                               ident[0:CW[c], 0:CW[c]])
                    if k == KD - 1:
                        last.then_inc(s_cps, 1)
                    yield

            def transpose_rows(src, signal):
                for k in range(KD):
                    last = nc.tensor.transpose(p_t[:, T * k:T * k + T], src[:, P * k:P * k + P], ident[0:T, 0:T])
                last.then_inc(signal, 1)

            def logits(b):
                pe.wait_ge(s_tT, b + 1)
                for k in range(KD):
                    last = nc.tensor.matmul(p_lg[0:T, 0:E], tT[:, k, :], rw[:, k, :],
                                            start=(k == 0), stop=(k == KD - 1))
                    if k == KD - 1:
                        last.then_inc(s_lgps, 1)
                    yield

            def ranks(b):
                pe.wait_ge(s_hot, b + 1)
                pe.wait_ge(s_sum, b + 1)
                nc.tensor.matmul(p_rk[0:T, 0:E], tri, hot[:, :], start=True, stop=False)
                nc.tensor.matmul(p_rk[0:T, 0:E], ones[0:T, 0:T], hot_sum[:, :],
                                 start=False, stop=True).then_inc(s_rkps, 1)
                yield

            def run(*work):
                for w in work:
                    for _ in w:
                        pass

            def step(b, rnd, place, first, last_batch):
                nxt = (place + 1) % RING
                pe.wait_ge(s_ctxD, b + 1)
                pe.wait_ge(s_ctxA, 5 * b + 5)
                pe.wait_ge(s_xnT, b + 1)
                if not first:
                    pe.wait_ge(s_hidT, b)
                if not last_batch:
                    pe.wait_ge(s_ctx[nxt], 32 * (rnd + (place + 1) // RING) + 32)
                    small = chain(*(context_transposes(nxt, c) for c in range(3)))
                else:
                    small = iter(())
                for i, (dst, lo, hi) in enumerate(((p_xa, 0, SA), (p_xb, SA, S))):
                    for k in range(KD):
                        last = nc.tensor.matmul(dst[0:T, 0:hi - lo], xnT[:, k, :], ctxT[:, k, lo:hi],
                                                start=(k == 0), stop=(k == KD - 1))
                        if i == 1 and k == KD - 1:
                            last.then_inc(s_x1ps, 1)
                        next(small, None)
                        if k % 2:
                            next(small, None)
                run(small)
                if not first:
                    pe.wait_ge(s_t, b)
                    transpose_rows(tn, s_tps)
                if not last_batch:
                    pe.wait_ge(s_ctxD, b + 2)
                    run(context_transposes(nxt, 3))
                pe.wait_ge(s_hid, b + 1)
                for c in range(SC):
                    last = nc.tensor.transpose((p_xa if c < 3 else p_xb)[0:CW[c], T * (c % 3):T * (c % 3) + T],
                                               hid[:, P * c:P * c + CW[c]], ident[0:T, 0:T])
                last.then_inc(s_hps, 1)
                if not last_batch:
                    pe.wait_ge(s_ctxA, 5 * b + 6)
                    run(context_transposes(nxt, 4))
                    pe.wait_ge(s_xn, b + 2)
                    if not first:
                        pe.wait_ge(s_tT, b)
                    transpose_rows(xn, s_xnps)
                pe.wait_ge(s_hidT, b + 1)
                if not last_batch:
                    pe.wait_ge(s_ctxA, 5 * b + 7)
                early = [iter(()) if first else logits(b - 1), iter(()) if last_batch else context_transposes(nxt, 5)]
                for c in range(SC):
                    last = nc.tensor.matmul(p_att[0:T, :], hidT[0:CW[c], c, :], cxs[place][0:CW[c], c, :],
                                            start=(c == 0), stop=(c == SC - 1))
                    if c == SC - 1:
                        last.then_inc(s_att, 1)
                    if c < 2:
                        next(early[0], None)
                        next(early[0], None)
                    elif c < 4:
                        next(early[1], None)
                        next(early[1], None)
                    elif c == 4 and not first:
                        run(early[0], ranks(b - 1))
                run(*early)

            pe.wait_ge(s_con, 48)
            pe.wait_ge(s_ctx[0], 32)
            for c in range(SC):
                if c == 3:
                    pe.wait_ge(s_ctxD, 1)
                if c > 3:
                    pe.wait_ge(s_ctxA, c - 3)
                run(context_transposes(0, c))
            pe.wait_ge(s_xn, 1)
            transpose_rows(xn, s_xnps)
            batches(pe, step)
            pe.wait_ge(s_t, NB)
            transpose_rows(tn, s_tps)
            run(logits(NB - 1))
            run(ranks(NB - 1))
            pe.wait_ge(s_sum, NB + 1)
            nc.tensor.matmul(p_lg[:, 0:E], ones[0:T, :], hot_sum[:, :], start=True, stop=True
                             ).then_inc(s_cntps, 1)
            pe.wait_ge(s_blkhot, 1)
            for h in range(2):
                for b in range(NB):
                    last = nc.tensor.matmul(p_rk[BLK * h:BLK * h + BLK, 0:NCOL], row_hot[:, b, :], blk_hot[:, b, :],
                                            start=(b == 0), stop=(b == NB - 1))
            last.then_inc(s_idps, 1)

            def transpose_from(j, par, used_sem):
                buf = g_t[par]
                pe.wait_ge(s_gt[par], 8 * j + (16 - 8 * par))
                for k in range(KD):
                    last = nc.tensor.transpose(p_blk[:, P * k:P * k + P], buf[:, P * k:P * k + P], ident)
                    if k == 0 and used_sem is not None:
                        last.then_inc(used_sem, 1)
                last.then_inc(s_bps, 1)

            def transpose_block(j, used_sem=None):
                if isinstance(j, int):
                    transpose_from(j, j % 2, used_sem)
                else:
                    with pe.If(pe.snap(j % 2) > 0):
                        transpose_from(j, 1, used_sem)
                    with pe.Else():
                        transpose_from(j, 0, used_sem)

            def second_layer(j, slot):
                pe.wait_ge(s_act, j + 1)
                for c in range(KF):
                    for h in range(2):
                        last = nc.tensor.matmul(p_y[BLK * h:BLK * h + BLK, 0:HD], hT[:, 2 * (c % 4) + c // 4, :],
                                                W2[:, slot, c, HD * h:HD * h + HD],
                                                start=(c == 0), stop=(c == KF - 1))
                last.then_inc(s_y, 1)

            def unit(j, e, rnd, slot, before_slot, first):
                pe.wait_ge(s_blkT, j + 1)
                if first:
                    pe.wait_ge(s_w1[slot], 32 * rnd + 32)
                if before_slot is not None:
                    pe.wait_ge(s_hc, j)
                for k in range(KD):
                    for h in range(2):
                        last = nc.tensor.matmul(p_h[BLK * h:BLK * h + BLK, :], blkT[:, k, :],
                                                W1[:, slot, k, D * h:D * h + D],
                                                start=(k == 0), stop=(k == KD - 1))
                last.then_inc(s_hp, 1)
                transpose_block(j + 1, s_w1_used if first else None)
                if before_slot is not None:
                    second_layer(j - 1, before_slot)
                pe.wait_ge(s_hc, j + 1)
                for c in range(4):
                    last = nc.tensor.transpose(p_hT[:, P * c:P * c + P], h_pre[:, P * c:P * c + P], ident)
                    if c == 0 and first and before_slot is not None:
                        last.then_inc(s_w2_used, 1)
                last.then_inc(s_hTp, 1)
                if first:
                    pe.wait_ge(s_w2[slot], 32 * rnd + 32)

            pe.wait_ge(s_table, 1)
            transpose_block(0)
            last = blocks_of_experts(pe, unit)
            second_layer(last, (E - 1) % SLOTS)

        @block.scalar
        def _(act):
            def copy_context(b, groups):
                for c in groups:
                    act.wait_ge(s_cps, SC * b + (c + 1))
                    nc.scalar.copy(ctxT[:, :, P * c:P * c + CW[c]],
                                   p_c[c % 3][:, :].rearrange("p (k f) -> p k f", k=KD)[:, :, 0:CW[c]]
                                   ).then_inc(s_ctxA, 1)

            def copy_rows(dst, wait, signal, b):
                act.wait_ge(wait, b + 1)
                nc.scalar.copy(dst[:, :, :], p_t[:, 0:KD * T].rearrange("p (k t) -> p k t", k=KD)).then_inc(signal, 1)

            def gate_tanh(b):
                act.wait_ge(s_top, b + 1)
                nc.scalar.activation(gate[:, :], top[:, :], ACT.Tanh, scale=0.5).then_inc(s_tanh, 1)

            def step(b, rnd, place, first, last_batch):
                act.wait_ge(s_x1ps, b + 1)
                nc.scalar.activation(hid[:, 0:SA], p_xa[0:T, 0:SA], ACT.Gelu_apprx_tanh).then_inc(s_gelu, 1)
                nc.scalar.activation(hid[:, SA:S], p_xb[0:T, 0:S - SA], ACT.Gelu_apprx_tanh).then_inc(s_gelu, 1)
                if not last_batch:
                    copy_context(b + 1, (1, 2))
                if not first:
                    copy_rows(tT, s_tps, s_tT, b - 1)
                if not last_batch:
                    copy_context(b + 1, (3,))
                act.wait_ge(s_hps, b + 1)
                nc.scalar.copy(hidT[:, 0:3, :], p_xa[:, 0:3 * T].rearrange("p (c t) -> p c t", c=3))
                nc.scalar.copy(hidT[:, 3:5, :], p_xb[:, 0:2 * T].rearrange("p (c t) -> p c t", c=2))
                nc.scalar.copy(hidT[0:CW[5], 5, :], p_xb[0:CW[5], 2 * T:3 * T]).then_inc(s_hidT, 1)
                if not last_batch:
                    copy_context(b + 1, (4,))
                    copy_rows(xnT, s_xnps, s_xnT, b + 1)
                    copy_context(b + 1, (5,))
                if not first:
                    gate_tanh(b - 1)

            copy_context(0, range(1, SC))
            copy_rows(xnT, s_xnps, s_xnT, 0)
            batches(act, step)
            copy_rows(tT, s_tps, s_tT, NB - 1)
            gate_tanh(NB - 1)

            def copy_block(j):
                act.wait_ge(s_bps, j + 1)
                nc.scalar.copy(blkT[:, :, :], p_blk[:, :].rearrange("p (k t) -> p k t", k=KD)[:, :, 0:BLK]).then_inc(s_blkT, 1)

            act.wait_ge(s_table, 1)
            n = last_block(act) + 1
            copy_block(0)
            with act.Fori(0, n) as j:
                copy_block(j + 1)
                act.wait_ge(s_hb, j + 1)
                nc.scalar.activation(hT[:, :, :], hT[:, :, :], ACT.Gelu).then_inc(s_act, 1)

        @block.vector
        def _(dve):
            def apart():
                dve.sem_inc(s_apart_v, 1)

            def norm(b, src, bn, ag, ve, rs, s_bn, s_ag, s_ve, s_rs, dst, signal):
                nc.vector.bn_stats(bn[:, :], src).then_inc(s_bn, 1)
                dve.wait_ge(s_bn, b + 1)
                apart()
                nc.vector.bn_aggr(ag[:, :], bn[:, :]).then_inc(s_ag, 1)
                dve.wait_ge(s_ag, b + 1)
                nc.vector.tensor_scalar(ve[:, :], ag[:, 1:2], EPS, None, ALU.add).then_inc(s_ve, 1)
                dve.wait_ge(s_rs, b + 1)
                nc.vector.tensor_scalar(dst, src, ag[:, 0:1], rs[:, 0:1], ALU.subtract, ALU.mult).then_inc(signal, 1)

            def norm_x(b, rnd, place):
                dve.wait_ge(s_x[place], 16 * rnd + 16)
                norm(b, xin[:, place, :], bn_x, ag_x, ve_x, rs_x, s_bnx, s_agx, s_vex, s_rsx, xn[:, :], s_xn)

            def route(b):
                dve.wait_ge(s_lgps, b + 1)
                nc.vector.tensor_reduce(top[:, :], p_lg[0:T, 0:E], AX.X, ALU.max).then_inc(s_top, 1)
                dve.wait_ge(s_top, b + 1)
                nc.vector.scalar_tensor_tensor(out=cand[:, :], in0=p_lg[0:T, 0:E], scalar=top[:, 0:1], in1=e_low,
                                               op0=ALU.is_ge, op1=ALU.mult).then_inc(s_cand, 1)
                dve.wait_ge(s_cand, b + 1)
                nc.vector.tensor_reduce(who[:, :], cand[:, :], AX.X, ALU.min).then_inc(s_who, 1)
                dve.wait_ge(s_who, b + 1)
                nc.vector.tensor_scalar(hot[:, :], e_low, who[:, 0:1], None, ALU.is_equal).then_inc(s_hot, 1)
                here = hot_all[:, bass.ds(b, 1), :].rearrange("p o e -> p (o e)")
                nc.vector.tensor_scalar(here, e_low, who[:, 0:1], None, ALU.is_equal).then_inc(s_rowhot, 1)

            def rank_and_gate(b, place):
                dve.wait_ge(s_rkps, b + 1)
                nc.vector.tensor_tensor_reduce(rank_tmp[:, :], p_rk[0:T, 0:E], hot[:, :], 1.0, 0.0,
                                               ALU.mult, ALU.add, rank[:, :]).then_inc(s_rank, 1)
                nc.vector.tensor_tensor(hot_sum[:, :], hot_sum[:, :], hot[:, :], ALU.add).then_inc(s_sum, 1)
                dve.wait_ge(s_rank, b + 1)
                nc.vector.tensor_scalar(over[:, :], thr[0:T], rank[:, 0:1], None, ALU.is_le).then_inc(s_over, 1)
                dve.wait_ge(s_over, b + 1)
                nc.vector.tensor_reduce(quot[:, :], over[:, :], AX.X, ALU.add).then_inc(s_quot, 1)
                dve.wait_ge(s_quot, b + 1)
                nc.vector.scalar_tensor_tensor(out=rest[:, :], in0=quot[:, :], scalar=-float(BLK), in1=rank[:, :],
                                               op0=ALU.mult, op1=ALU.add).then_inc(s_rest, 1)
                nc.vector.tensor_scalar(quot_all[:, bass.ds(b, 1)], quot[:, :], 1.0, None, ALU.mult)
                dve.wait_ge(s_rest, b + 1)
                here = row_hot[:, bass.ds(b, 1), :].rearrange("p o n -> p (o n)")
                nc.vector.tensor_scalar(here, rows64, rest[:, 0:1], None, ALU.is_equal).then_inc(s_rowhot, 1)
                dve.wait_ge(s_tanh, b + 1)
                nc.vector.tensor_scalar(xw[:, place, 0, HD:XW], gate[:, :], 0.5, 0.5, ALU.mult, ALU.add)
                nc.vector.tensor_scalar(xw[:, place, 1, HD:XW], gate[:, :], 0.5, 0.5, ALU.mult, ALU.add
                                        ).then_inc(s_gate, 1)

            def copy_context(b):
                dve.wait_ge(s_cps, SC * b + 1)
                nc.vector.tensor_copy(ctxT[:, :, 0:P], p_c[0][:, :].rearrange("p (k f) -> p k f", k=KD)
                                      ).then_inc(s_ctxD, 1)

            def step(b, rnd, place, first, last_batch):
                if not last_batch:
                    dve.wait_ge(s_xnps, b + 1)
                    norm_x(b + 1, rnd + (place + 1) // RING, (place + 1) % RING)
                    dve.wait_ge(s_x1ps, b + 1)
                    copy_context(b + 1)
                dve.wait_ge(s_gelu, 2 * b + 1)
                nc.vector.tensor_tensor(hid[:, 0:SA], hid[:, 0:SA], p_xa[0:T, 0:SA], ALU.mult)
                dve.wait_ge(s_gelu, 2 * b + 2)
                nc.vector.tensor_tensor(hid[:, SA:S], hid[:, SA:S], p_xb[0:T, 0:S - SA], ALU.mult).then_inc(s_hid, 1)
                if not first:
                    route(b - 1)
                    rank_and_gate(b - 1, (place - 1) % RING)
                dve.wait_ge(s_att, b + 1)
                dve.wait_ge(s_xwrow[place], 16 * rnd + 16)
                x2 = xw[:, place, :, 0:HD]
                nc.vector.tensor_tensor(x2, xin[:, place, :].rearrange("p (h d) -> p h d", h=2),
                                        p_att[0:T, :].rearrange("p (h d) -> p h d", h=2), ALU.add).then_inc(s_x2, 1)
                dve.wait_ge(s_x2, b + 1)
                dve.wait_ge(s_trow, 16 * b + 16)
                norm(b, x2, bn_t, ag_t, ve_t, rs_t, s_bnt, s_agt, s_vet, s_rst,
                     tn[:, :].rearrange("p (h d) -> p h d", h=2), s_t)

            nc.vector.memset(hot_sum[:, :], 0.0).then_inc(s_sum, 1)
            dve.wait_ge(s_con, 48)
            norm_x(0, 0, 0)
            copy_context(0)
            batches(dve, step)
            route(NB - 1)
            rank_and_gate(NB - 1, (NB - 1) % RING)

            dve.wait_ge(s_cntps, 1)
            nc.vector.tensor_tensor(cnt_over, p_lg[:, 0:E].unsqueeze(2).to_broadcast([P, E, NTHR]),
                                    thr.unsqueeze(1).to_broadcast([P, E, NTHR]), ALU.is_gt).then_inc(s_table2, 1)
            dve.wait_ge(s_table2, 1)
            nc.vector.tensor_reduce(extra[:, :], cnt_over, AX.X, ALU.add).then_inc(s_table2, 1)
            dve.wait_ge(s_table2, 2)
            nc.vector.tensor_tensor(before, extra[:, :].unsqueeze(1).to_broadcast([P, E, E]), e_before, ALU.mult
                                    ).then_inc(s_table2, 1)
            dve.wait_ge(s_table2, 3)
            nc.vector.tensor_reduce(start[:, :], before, AX.X, ALU.add).then_inc(s_table2, 1)
            dve.wait_ge(s_table2, 4)
            nc.vector.tensor_tensor(start[:, :], start[:, :], e_num, ALU.add).then_inc(s_table2, 1)
            dve.wait_ge(s_table2, 5)
            dve.wait_ge(s_rowhot, 2 * NB)
            nc.vector.tensor_tensor(start_tok, hot_all[:, :, :], start[0:T, :].unsqueeze(1).to_broadcast([T, NB, E]),
                                    ALU.mult).then_inc(s_table2, 1)
            nc.vector.scalar_tensor_tensor(out=ends[:, 0:E], in0=start[:, :], scalar=1.0, in1=extra[:, :],
                                           op0=ALU.add, op1=ALU.add)
            nc.vector.tensor_tensor(ends[:, E:E + 1], start[:, E - 1:E], extra[:, E - 1:E], ALU.add
                                    ).then_inc(s_table, 1)
            dve.wait_ge(s_table2, 6)
            nc.vector.tensor_reduce(blk_of[:, :], start_tok, AX.X, ALU.add).then_inc(s_table2, 1)
            dve.wait_ge(s_table2, 7)
            nc.vector.tensor_tensor(blk_of[:, :], blk_of[:, :], quot_all[:, :], ALU.add).then_inc(s_table2, 1)
            dve.wait_ge(s_table2, 8)
            nc.vector.tensor_tensor(blk_hot, blks.unsqueeze(1).to_broadcast([T, NB, NCOL]),
                                    blk_of[:, :].unsqueeze(2).to_broadcast([T, NB, NCOL]), ALU.is_equal
                                    ).then_inc(s_table2, 1)
            dve.wait_ge(s_table2, 9)
            nc.vector.tensor_tensor(blk_hot, blk_hot, tok_low.unsqueeze(2).to_broadcast([T, NB, NCOL]), ALU.mult
                                    ).then_inc(s_blkhot, 1)
            dve.wait_ge(s_idps, 1)
            nc.vector.tensor_scalar(id_tok[:, :], p_rk[:, 0:NCOL], float(TOK), None, ALU.add).then_inc(s_ids, 1)
            nc.vector.tensor_scalar(id_half[:, :], p_rk[:, 0:NCOL], 2.0, halves, ALU.mult, ALU.add).then_inc(s_ids, 1)

            def finish(j, slot):
                dve.wait_ge(s_y, j + 1)
                nc.vector.tensor_tensor(y_b, p_y[:, 0:HD], b2s[:, slot], ALU.add).then_inc(s_yb, 1)
                odd = dve.snap(j % 2) if not isinstance(j, int) else j % 2
                xg = g_x2[:, bass.ds(odd * XW, HD)]
                gates = g_x2[:, bass.ds(odd * XW + HD, 1)]
                yo = y_out2[:, bass.ds(odd * HD, HD)]
                dve.wait_ge(s_gx, 16 * j + 16)
                dve.wait_ge(s_y_free, j + 1)
                dve.wait_ge(s_yb, j + 1)
                nc.vector.scalar_tensor_tensor(out=yo, in0=y_b, scalar=gates, in1=xg,
                                               op0=ALU.mult, op1=ALU.add).then_inc(s_yo, 1)

            def unit(j, e, rnd, slot, before_slot, first):
                dve.wait_ge(s_hp, j + 1)
                nc.vector.tensor_copy(h_pre, p_h[:, :]).then_inc(s_hc, 1)
                if before_slot is not None:
                    finish(j - 1, before_slot)
                    if first:
                        dve.sem_inc(s_yb_used, 1)
                bias = b1s[:, bass.ds(e, 1), :].rearrange("p o c -> p (o c)").unsqueeze(2).to_broadcast([P, KF, BLK])
                if first:
                    dve.wait_ge(s_b2[slot], 32 * rnd + 32)
                dve.wait_ge(s_hTp, j + 1)
                nc.vector.tensor_tensor(hT[:, :, :], p_hT[:, :].rearrange("p (c t) -> p c t", c=KF), bias, ALU.add
                                        ).then_inc(s_hb, 1)

            dve.wait_ge(s_table, 1)
            last = blocks_of_experts(dve, unit)
            finish(last, (E - 1) % SLOTS)

        @block.gpsimd
        def _(pool):
            def apart():
                pool.sem_inc(s_apart_p, 1)

            def inverse_root(b, ve, rs, s_ve, s_rs):
                pool.wait_ge(s_ve, b + 1)
                nc.gpsimd.tensor_tensor(rs[:, :], ve[:, :], neg_half, ALU.pow).then_inc(s_rs, 1)

            def step(b, rnd, place, first, last_batch):
                if not last_batch:
                    inverse_root(b + 1, ve_x, rs_x, s_vex, s_rsx)
                inverse_root(b, ve_t, rs_t, s_vet, s_rst)

            pool.sem_inc(s_trow, 16)
            for r in range(RING):
                pool.sem_inc(s_xwrow[r], 16)
            bound_t, bound_x = pool.to_reg(TOK - 1), pool.to_reg(2 * TOK - 1)
            pool.wait_ge(s_con, 48)
            inverse_root(0, ve_x, rs_x, s_vex, s_rsx)
            batches(pool, step)

            def column(j):
                return slice(j, j + 1) if isinstance(j, int) else bass.ds(j, 1)

            def gather_t(j, par):
                nc.gpsimd.tensor_copy(at_t[par][:, :], id_tok[:, column(j)]).then_inc(s_at_t, 1)
                pool.wait_ge(s_at_t, j + 1)
                apart()
                nc.gpsimd.indirect_dma_start(g_t[par][0:BLK], None, t_rows,
                                             bass.IndirectOffsetOnAxis(ap=at_t[par][0:BLK, :], axis=0),
                                             bounds_check=bound_t, oob_is_err=False).then_inc(s_gt[par], 16)

            def gather_x(j, par):
                nc.gpsimd.tensor_copy(at_x[par][:, :], id_half[:, column(j)]).then_inc(s_at_x, 1)
                pool.wait_ge(s_at_x, j + 1)
                apart()
                nc.gpsimd.indirect_dma_start(g_x[par], None, xw_rows,
                                             bass.IndirectOffsetOnAxis(ap=at_x[par][:, :], axis=0),
                                             bounds_check=bound_x, oob_is_err=False).then_inc(s_gx, 16)

            def scatter(j, par):
                nc.gpsimd.tensor_copy(at_out[par][:, :], id_half[:, column(j)]).then_inc(s_at_out, 1)
                pool.wait_ge(s_at_out, j + 1)
                pool.wait_ge(s_yo, j + 1)
                apart()
                nc.gpsimd.indirect_dma_start(out_halves, bass.IndirectOffsetOnAxis(ap=at_out[par][:, :], axis=0),
                                             y_out[par], None, bounds_check=bound_x, oob_is_err=False
                                             ).then_inc(s_done, 16)

            pool.wait_ge(s_idps, 1)
            for g in (*g_t, g_x2):
                nc.gpsimd.memset(g, 0.0).then_inc(s_g0, 1)
            pool.wait_ge(s_trow, 16 * NB + 16)
            pool.wait_ge(s_ids, 2)
            pool.wait_ge(s_g0, 3)
            gather_t(0, 0)
            gather_t(1, 1)
            for r in range(RING):
                pool.wait_ge(s_xwrow[r], 16 * (1 + len(range(r, NB, RING))))
            gather_x(0, 0)
            last = last_block(pool)

            def block_step(j, par, scatters=True):
                pool.wait_ge(s_bps, j + 1)
                apart()
                gather_t(j + 2, par)
                if scatters:
                    if not isinstance(j, int):
                        pool.wait_ge(s_done, 16 * (j - 1))
                    pool.sem_inc(s_y_free, 1)
                    scatter(j - 1, 1 - par)
                pool.wait_ge(s_gx, 16 * j + 16)
                apart()
                gather_x(j + 1, 1 - par)

            pool.sem_inc(s_y_free, 1)
            block_step(0, 0, scatters=False)
            block_step(1, 1)
            with pool.Fori(2, last + 1) as j:
                with pool.If(pool.snap(j % 2) > 0):
                    block_step(j, 1)
                with pool.Else():
                    block_step(j, 0)
            pool.wait_ge(s_done, 16 * last)
            apart()
            with pool.If(pool.snap(last % 2) > 0):
                scatter(last, 1)
            with pool.Else():
                scatter(last, 0)
            pool.wait_ge(s_done, 16 * last + 16)
            apart()
            with pool.If(pool.snap(last % 2) > 0):
                for par in range(2):
                    pool.wait_ge(s_gt[par], 8 * last + 24)
                pool.sem_inc(s_apart_p, 1)
            with pool.Else():
                pool.wait_ge(s_gt[0], 8 * last + 32)
                pool.wait_ge(s_gt[1], 8 * last + 16)
                pool.sem_inc(s_apart_p, 1)
            pool.wait_ge(s_gx, 16 * last + 32)


def kernel(x, ctx_1024, L0_ffn_router_w, L0_ffn_w1, L0_ffn_b1, L0_ffn_w2, L0_ffn_b2):
    import concourse.bacc as bacc
    from concourse.bass_utils import run_bass_kernel_spmd

    def laid(a, shape, order):
        return np.ascontiguousarray(np.transpose(np.reshape(np.asarray(a), shape), order))

    ctx = np.asarray(ctx_1024)
    full = P * (SC - 1)
    arrays = {
        "x": np.ascontiguousarray(x),
        "ctx_main": laid(ctx[:, 0:full], (NB, SC - 1, P, D), (0, 2, 1, 3)),
        "ctx_rest": np.ascontiguousarray(ctx[:, full:S]),
        "router": laid(L0_ffn_router_w, (KD, P, E), (1, 0, 2)),
        "w1": laid(L0_ffn_w1, (E, KD, P, F), (0, 2, 1, 3)),
        "b1": laid(L0_ffn_b1, (E, 2, 4, P), (3, 0, 2, 1)).reshape(P, E, KF),
        "w2": laid(L0_ffn_w2, (E, KF, P, D), (0, 2, 1, 3)),
        "b2": np.ascontiguousarray(L0_ffn_b2).reshape(E, 2, HD),
        "consts": shape_constants(),
    }
    nc = bacc.Bacc("TRN2", target_bir_lowering=False, num_devices=1)
    args = [nc.dram_tensor(f"in_{n}", a.shape, mybir.dt.from_np(a.dtype), kind="ExternalInput").ap()
            for n, a in arrays.items()]
    out = nc.dram_tensor("out", (NB, T, D), F32, kind="ExternalOutput").ap()
    build(nc, *args, out)
    r = run_bass_kernel_spmd(nc, [{f"in_{n}": a for n, a in arrays.items()}], core_ids=[0])
    return r.results[0]["out"]
```

```python
from contextlib import ExitStack
from itertools import chain

import numpy as np

import concourse.bass as bass
from concourse import mybir

F32 = mybir.dt.float32
I32 = mybir.dt.int32
U32 = mybir.dt.uint32
ALU = mybir.AluOpType
ACT = mybir.ActivationFunctionType
AX = mybir.AxisListType

P = 128
NB, T, D, S = 8, 100, 512, 722
E, F = 16, 1024
TOK = NB * T
KD = D // P
KF = F // P
SC = -(-S // P)
CW = [min(P, S - P * c) for c in range(SC)]
SA = 3 * P
BLK = 64
SMALL = 32
MAXB = E - 1 + -(-(TOK - E + 1) // BLK)
NCOL = MAXB + 6
NTHR = TOK // BLK
SLOTS = 5
RING = 3
HD = D // 2
XW = HD + 1
EPS = 1e-5

C_ID, C_NH, C_ONE = 0, P, P + 1
C_TRI = C_ONE + P
C_EM = C_TRI + T
C_THR = C_EM + E
C_PM = C_THR + NTHR
C_BLK = C_PM + BLK
C_TOK = C_BLK + NCOL
C_LT = C_TOK + NB
C_E = C_LT + E * E
C_HALF = C_E + E
C_ALL = C_HALF + 1


def shape_constants():
    c = np.zeros((P, C_ALL), np.float32)
    p = np.arange(P)
    c[:, C_ID:C_ID + P] = np.eye(P)
    c[:, C_ONE:C_ONE + P] = 1
    c[:, C_TRI:C_TRI + T] = p[:, None] < np.arange(T)
    c[:, C_EM:C_EM + E] = np.arange(E) - E
    c[:, C_THR:C_THR + NTHR] = BLK * (1 + np.arange(NTHR))
    c[:, C_PM:C_PM + BLK] = np.arange(BLK)
    c[:, C_BLK:C_BLK + NCOL] = np.arange(NCOL)
    c[:, C_TOK:C_TOK + NB] = p[:, None] + T * np.arange(NB) - TOK
    c[:, C_LT:C_LT + E * E] = (np.arange(E)[:, None] > np.arange(E)).ravel()
    c[:, C_E:C_E + E] = np.arange(E)
    c[:, C_HALF] = 2 * TOK + p // BLK
    c[:, C_NH] = -0.5
    return c


def build(nc, x, ctx_main, ctx_rest, router, w1, b1, w2, b2, consts, out):
    t_rows = nc.dram_tensor("t_rows", (TOK, D), F32).ap()
    xw_rows = nc.dram_tensor("xw_rows", (2 * TOK, XW), F32).ap()
    xw_by_token = xw_rows.rearrange("(n h) d -> n h d", h=2)
    out_halves = out.rearrange("b t (h d) -> (b t h) d", h=2)

    with ExitStack() as stack:
        def sb(name, shape, dt=F32):
            return stack.enter_context(nc.sbuf_tensor(name, shape, dt))

        def sem(name):
            return stack.enter_context(nc.semaphore(name))

        def sems(name, n):
            return [sem(f"{name}{i}") for i in range(n)]

        W1_early = sb("W1_early", [P, SLOTS - 1, KD, F])
        W2_early = sb("W2_early", [P, SLOTS - 1, KF, D])
        con = sb("con", [P, C_ALL])
        rw = sb("rw", [P, KD, E])
        b1s = sb("b1s", [P, E, KF])
        work = sb("work", [P, RING * SC * D])
        area = sb("area", [P, KD * S + RING * D])
        ctxT = area[:, 0:KD * S].rearrange("p (k s) -> p k s", k=KD)
        xin = area[0:T, KD * S:KD * S + RING * D].rearrange("p (r d) -> p r d", r=RING)
        xn = sb("xn", [T, D])
        xnT = sb("xnT", [P, KD, T])
        hid = sb("hid", [T, S])
        hidT = sb("hidT", [P, SC, T])
        xw = sb("xw", [T, RING, 2, XW])
        tn = sb("tn", [T, D])
        tT = sb("tT", [P, KD, T])
        bn_x, ag_x, ve_x, rs_x = sb("bn_x", [T, 6]), sb("ag_x", [T, 2]), sb("ve_x", [T, 1]), sb("rs_x", [T, 1])
        bn_t, ag_t, ve_t, rs_t = sb("bn_t", [T, 6]), sb("ag_t", [T, 2]), sb("ve_t", [T, 1]), sb("rs_t", [T, 1])
        top, cand, who, gate = sb("top", [T, 1]), sb("cand", [T, E]), sb("who", [T, 1]), sb("gate", [T, 1])
        hot, hot_sum, hot_all = sb("hot", [T, E]), sb("hot_sum", [T, E]), sb("hot_all", [T, NB, E])
        rank_tmp, rank, over = sb("rank_tmp", [T, E]), sb("rank", [T, 1]), sb("over", [T, NTHR])
        quot, quot_all, rest = sb("quot", [T, 1]), sb("quot_all", [T, NB]), sb("rest", [T, 1])
        row_hot = sb("row_hot", [T, NB, BLK])
        cnt_over = ctxT[:, 0, 0:E * NTHR].rearrange("p (e n) -> p e n", e=E)
        before = ctxT[:, 1, 0:E * E].rearrange("p (e n) -> p e n", e=E)
        start_tok = ctxT[0:T, 2, 0:NB * E].rearrange("p (b e) -> p b e", b=NB)
        blk_hot = ctxT[0:T, 3, 0:NB * NCOL].rearrange("p (b n) -> p b n", b=NB)
        extra, start, blk_of = sb("extra", [P, E]), sb("start", [P, E]), sb("blk_of", [T, NB])
        ends = sb("ends", [P, E + 1], I32)
        id_tok, id_half = sb("id_tok", [P, NCOL], U32), sb("id_half", [P, NCOL], U32)
        at_t, at_x, at_out = ([sb(f"{n}{i}", [P, 1], U32) for i in range(2)] for n in ("at_t", "at_x", "at_out"))

        cxs = [work[:, SC * D * i:SC * D * (i + 1)].rearrange("p (c d) -> p c d", c=SC) for i in range(RING)]
        used = [0]

        def part2(n):
            used[0] += n
            assert used[0] <= RING * SC * D
            return work[:, used[0] - n:used[0]]
        g_t = [part2(D) for _ in range(2)]
        g_x2 = part2(2 * XW)
        g_x = [g_x2[:, XW * i:XW * i + XW] for i in range(2)]
        pairT = part2(KD * P).rearrange("p (k t) -> p k t", k=KD)
        h_pre = part2(D)
        hT = part2(KF * BLK).rearrange("p (c t) -> p c t", c=KF)
        y_b = area[:, KF * D:KF * D + HD]
        y_out2 = part2(2 * HD)
        y_out = [y_out2[:, HD * i:HD * i + HD] for i in range(2)]
        b2s = part2(SLOTS * HD).rearrange("p (s d) -> p s d", s=SLOTS)
        W1 = [W1_early[:, s] for s in range(SLOTS - 1)] + [part2(KD * F).rearrange("p (k f) -> p k f", k=KD)]
        W2 = ([W2_early[:, s] for s in range(SLOTS - 1)]
              + [area[:, 0:KF * D].rearrange("p (k d) -> p k d", k=KF)])

        ident, ones = con[:, C_ID:C_ID + P], con[:, C_ONE:C_ONE + P]
        tri, e_low = con[0:T, C_TRI:C_TRI + T], con[0:T, C_EM:C_EM + E]
        thr = con[:, C_THR:C_THR + NTHR]
        rows64, blks = con[0:T, C_PM:C_PM + BLK], con[0:T, C_BLK:C_BLK + NCOL]
        tok_low = con[0:T, C_TOK:C_TOK + NB]
        e_before = con[:, C_LT:C_LT + E * E].rearrange("p (e n) -> p e n", e=E)
        e_num, halves, neg_half = con[:, C_E:C_E + E], con[:, C_HALF:C_HALF + 1], con[0:T, C_NH:C_NH + 1]

        bank = [stack.enter_context(nc.psum_tensor(f"bank{i}", [P, 512], F32)) for i in range(8)]
        p_xa, p_xb, p_t, p_att, p_lg = bank[0], bank[1], bank[2], bank[6], bank[7]
        p_rk = p_lg[:, 64:128]
        p_c = bank[3:6]
        p_h, p_hT, p_blk, p_y = bank[0], bank[1], bank[2], bank[5]

        s_con0, s_con, s_ctx_first = sem("s_con0"), sem("s_con"), sem("s_ctx_first")
        s_x, s_ctx = sems("s_x_in", RING), sems("s_ctx", RING)
        s_w1, s_w2 = ([sems(f"{n}_{i}_", 2) for i in range(SLOTS)] for n in ("s_w1", "s_w2"))
        s_b2 = sems("s_b2", SLOTS)
        s_trow, s_xwrow = sem("s_trow"), sems("s_xwrow", RING)
        s_x1ps, s_tps, s_cps, s_lgps = sem("s_x1ps"), sem("s_tps"), sem("s_cps"), sem("s_lgps")
        s_hps, s_xnps, s_att, s_rkps = sem("s_hps"), sem("s_xnps"), sem("s_att"), sem("s_rkps")
        s_cntps, s_idps = sem("s_cntps"), sem("s_idps")
        s_gelu, s_tT, s_ctxA, s_hidT = sem("s_gelu"), sem("s_tT"), sem("s_ctxA"), sem("s_hidT")
        s_tanh, s_xnT = sem("s_tanh"), sem("s_xnT")
        s_ctxD = sem("s_ctxD")
        s_bnx, s_agx, s_vex, s_rsx, s_xn = (sem(n) for n in ("s_bnx", "s_agx", "s_vex", "s_rsx", "s_xn"))
        s_bnt, s_agt, s_vet, s_rst, s_t = (sem(n) for n in ("s_bnt", "s_agt", "s_vet", "s_rst", "s_t"))
        s_hid, s_x2, s_top, s_cand, s_who, s_hot = (
            sem(n) for n in ("s_hid", "s_x2", "s_top", "s_cand", "s_who", "s_hot"))
        s_sum, s_rank, s_over, s_quot, s_rest, s_rowhot, s_gate = (
            sem(n) for n in ("s_sum", "s_rank", "s_over", "s_quot", "s_rest", "s_rowhot", "s_gate"))
        s_table, s_blkhot, s_ids, s_g0 = sem("s_table"), sem("s_blkhot"), sem("s_ids"), sem("s_g0")
        s_table2, s_yb_used, s_y_free = sem("s_table2"), sem("s_yb_used"), sem("s_y_free")
        s_hT0 = sem("s_hT0")
        s_apart_v, s_apart_p = sem("s_apart_v"), sem("s_apart_p")
        s_bps, s_hp, s_hTp, s_y = sem("s_bps"), sem("s_hp"), sem("s_hTp"), sem("s_y")
        s_w1_used, s_w2_used = sem("s_w1_used"), sem("s_w2_used")
        s_pairT, s_act = sem("s_pairT"), sem("s_act")
        s_hc, s_hb, s_yb, s_yo = sem("s_hc"), sem("s_hb"), sem("s_yb"), sem("s_yo")
        s_at_t, s_at_x, s_at_out = sem("s_at_t"), sem("s_at_x"), sem("s_at_out")
        s_gt, s_gx, s_done = sems("s_gt", 2), sem("s_gx"), sems("s_done", 2)

        block = stack.enter_context(nc.Block())

        def batches(eng, step):
            step(0, 0, 0, True, False)
            with eng.Fori(0, (NB - 2) // RING) as i:
                for u in range(RING):
                    step(RING * i + (1 + u), i + (1 + u) // RING, (1 + u) % RING, False, False)
            step(NB - 1, (NB - 1) // RING, (NB - 1) % RING, False, True)

        def by_parity(eng, j, step):
            with eng.If(eng.snap(j % 2) > 0):
                step(1)
            with eng.Else():
                step(0)

        def by_size(eng, j, body):
            at = slice(j, j + 1) if isinstance(j, int) else bass.ds(j, 1)
            row = eng.value_load(id_half[SMALL:SMALL + 1, at], min_val=0, max_val=2 * TOK)
            with eng.If(row < 2 * TOK):
                body(True)
            with eng.Else():
                body(False)

        def last_block(eng):
            return eng.value_load(ends[0:1, E:E + 1], min_val=E - 1, max_val=MAXB - 1)

        def blocks_of_experts(eng, unit):
            def rest_of(e, rnd, slot, first, end):
                with eng.If(end > first + 1):
                    with eng.Fori(first + 1, end) as j:
                        unit(j, e, rnd, slot, slot, False)

            end = eng.value_load(ends[0:1, 0:1], min_val=1, max_val=MAXB - E + 1)
            unit(0, 0, 0, 0, None, True)
            rest_of(0, 0, 0, 0, end)
            with eng.Fori(0, (E - 1) // SLOTS) as g:
                first = eng.value_load(ends[0:1, bass.ds(SLOTS * g, 1)], min_val=1, max_val=MAXB - 1)
                for s in range(SLOTS):
                    e, rnd, slot = SLOTS * g + (1 + s), g + (1 + s) // SLOTS, (1 + s) % SLOTS
                    end = eng.value_load(ends[0:1, bass.ds(e, 1)], min_val=2, max_val=MAXB)
                    unit(first, e, rnd, slot, (slot - 1) % SLOTS, True)
                    rest_of(e, rnd, slot, first, end)
                    first = end
            assert (E - 1) % SLOTS == 0
            return last_block(eng)

        @block.sync
        def _(sp):
            def load_batch(b):
                r = b % RING
                sp.dma_start(xin[:, r, :], x[b]).then_inc(s_x[r], 16)
                sp.dma_start(cxs[r][:, 0:SC - 1, :], ctx_main[b]).then_inc(s_ctx[r], 16)
                sp.dma_start(cxs[r][0:CW[-1], SC - 1, :], ctx_rest[b]).then_inc(s_ctx[r], 16)

            def load_half(dst, src, signals, h):
                n = dst.shape[1] // 2
                sp.dma_start(dst[:, n * h:n * h + n], src[:, n * h:n * h + n]).then_inc(signals[h], 16)

            def load_layer(dst, src, signals):
                for h in range(2):
                    load_half(dst, src, signals, h)

            sp.dma_start(con[:, 0:C_ONE], consts[:, 0:C_ONE]).then_inc(s_con0, 16)
            sp.dma_start(cxs[0][:, 0:2, :], ctx_main[0][:, 0:2]).then_inc(s_ctx_first, 16)
            sp.dma_start(xin[:, 0, :], x[0]).then_inc(s_x[0], 16)
            sp.dma_start(cxs[0][:, 2:SC - 1, :], ctx_main[0][:, 2:SC - 1]).then_inc(s_ctx[0], 16)
            sp.dma_start(cxs[0][0:CW[-1], SC - 1, :], ctx_rest[0]).then_inc(s_ctx[0], 16)
            sp.dma_start(con[:, C_ONE:C_ALL], consts[:, C_ONE:C_ALL]).then_inc(s_con, 16)
            sp.dma_start(rw[:, :, :], router).then_inc(s_con, 16)
            sp.dma_start(b1s[:, :, :], b1).then_inc(s_con, 16)
            load_batch(1)
            load_batch(2)
            for b in range(NB):
                if b // 2 < SLOTS - 1:
                    W, w, signal = (W1, w1, s_w1) if b % 2 == 0 else (W2, w2, s_w2)
                    load_layer(W[b // 2], w[b // 2], signal[b // 2])
                if b == NB - 1:
                    sp.wait_ge(s_att, NB)
                    load_layer(W1[SLOTS - 1], w1[SLOTS - 1], s_w1[SLOTS - 1])
                    for s in range(SLOTS):
                        for h in range(2):
                            sp.dma_start(b2s[BLK * h:BLK * h + BLK, s], b2[s, h].partition_broadcast(BLK)
                                         ).then_inc(s_b2[s], 16)
                sp.wait_ge(s_t, b + 1)
                sp.dma_start(t_rows[T * b:T * b + T, :], tn[:, :]).then_inc(s_trow, 16)
                if b + RING < NB:
                    sp.wait_ge(s_att, b + 1)
                    sp.wait_ge(s_x2, b + 1)
                    load_batch(b + RING)
                sp.wait_ge(s_gate, b + 1)
                sp.dma_start(xw_by_token[T * b:T * b + T], xw[:, b % RING]).then_inc(s_xwrow[b % RING], 16)
            sp.wait_ge(s_x2, NB)
            sp.wait_ge(s_idps, 1)
            sp.wait_ge(s_bps, 1)
            load_layer(W2[SLOTS - 1], w2[SLOTS - 1], s_w2[SLOTS - 1])

            def load_expert(e, rnd, s):
                one = slice(e, e + 1) if isinstance(e, int) else bass.ds(e, 1)
                first, second = (w[one].rearrange("o p k f -> (o p) k f") for w in (w1, w2))
                before = (s - 1) % SLOTS
                in_before = 16 * (rnd + (s - 1) // SLOTS) + 16
                sp.wait_ge(s_w1_used, e - (SLOTS - 2))
                sp.wait_ge(s_w2[before][0], in_before)
                load_half(W1[s], first, s_w1[s], 0)
                sp.wait_ge(s_w2[before][1], in_before)
                load_half(W1[s], first, s_w1[s], 1)
                sp.wait_ge(s_w2_used, e - (SLOTS - 1))
                sp.wait_ge(s_w1[s][0], 16 * rnd + 16)
                load_half(W2[s], second, s_w2[s], 0)
                sp.wait_ge(s_w1[s][1], 16 * rnd + 16)
                load_half(W2[s], second, s_w2[s], 1)
                sp.wait_ge(s_yb_used, e - (SLOTS - 1))
                for h in range(2):
                    sp.dma_start(b2s[BLK * h:BLK * h + BLK, s], b2[one, h].partition_broadcast(BLK)
                                 ).then_inc(s_b2[s], 16)

            with sp.Fori(1, E // SLOTS) as g:
                for s in range(SLOTS):
                    load_expert(SLOTS * g + s, g, s)
            assert E % SLOTS == 1
            load_expert(E - 1, E // SLOTS, 0)

        @block.tensor
        def _(pe):
            def context_transposes(place, c):
                for k in range(KD):
                    last = nc.tensor.transpose(p_c[c % 3][:, P * k:P * k + CW[c]],
                                               cxs[place][0:CW[c], c, P * k:P * k + P],
                                               ident[0:CW[c], 0:CW[c]])
                    if k == KD - 1:
                        last.then_inc(s_cps, 1)
                    yield

            def transpose_rows(src, signal):
                for k in range(KD):
                    last = nc.tensor.transpose(p_t[:, T * k:T * k + T], src[:, P * k:P * k + P], ident[0:T, 0:T])
                last.then_inc(signal, 1)

            def logits(b):
                pe.wait_ge(s_tT, b + 1)
                for k in range(KD):
                    last = nc.tensor.matmul(p_lg[0:T, 0:E], tT[:, k, :], rw[:, k, :],
                                            start=(k == 0), stop=(k == KD - 1))
                    if k == KD - 1:
                        last.then_inc(s_lgps, 1)
                    yield

            def ranks(b):
                pe.wait_ge(s_hot, b + 1)
                pe.wait_ge(s_sum, b + 1)
                nc.tensor.matmul(p_rk[0:T, 0:E], tri, hot[:, :], start=True, stop=False)
                nc.tensor.matmul(p_rk[0:T, 0:E], ones[0:T, 0:T], hot_sum[:, :],
                                 start=False, stop=True).then_inc(s_rkps, 1)
                yield

            def run(*work):
                for w in work:
                    for _ in w:
                        pass

            def step(b, rnd, place, first, last_batch):
                nxt = (place + 1) % RING
                pe.wait_ge(s_ctxD, b + 1)
                pe.wait_ge(s_ctxA, 5 * b + 5)
                pe.wait_ge(s_xnT, b + 1)
                if not first:
                    pe.wait_ge(s_hidT, b)
                if not last_batch:
                    pe.wait_ge(s_ctx[nxt], 32 * (rnd + (place + 1) // RING) + 32)
                    small = chain(*(context_transposes(nxt, c) for c in range(3)))
                else:
                    small = iter(())
                for i, (dst, lo, hi) in enumerate(((p_xa, 0, SA), (p_xb, SA, S))):
                    for k in range(KD):
                        last = nc.tensor.matmul(dst[0:T, 0:hi - lo], xnT[:, k, :], ctxT[:, k, lo:hi],
                                                start=(k == 0), stop=(k == KD - 1))
                        if i == 1 and k == KD - 1:
                            last.then_inc(s_x1ps, 1)
                        next(small, None)
                        if k % 2:
                            next(small, None)
                run(small)
                if not first:
                    pe.wait_ge(s_t, b)
                    transpose_rows(tn, s_tps)
                if not last_batch:
                    pe.wait_ge(s_ctxD, b + 2)
                    run(context_transposes(nxt, 3))
                pe.wait_ge(s_hid, b + 1)
                for c in range(SC):
                    last = nc.tensor.transpose((p_xa if c < 3 else p_xb)[0:CW[c], T * (c % 3):T * (c % 3) + T],
                                               hid[:, P * c:P * c + CW[c]], ident[0:T, 0:T])
                last.then_inc(s_hps, 1)
                if not last_batch:
                    pe.wait_ge(s_ctxA, 5 * b + 6)
                    run(context_transposes(nxt, 4))
                    pe.wait_ge(s_xn, b + 2)
                    if not first:
                        pe.wait_ge(s_tT, b)
                    transpose_rows(xn, s_xnps)
                pe.wait_ge(s_hidT, b + 1)
                if not last_batch:
                    pe.wait_ge(s_ctxA, 5 * b + 7)
                early = [iter(()) if first else logits(b - 1), iter(()) if last_batch else context_transposes(nxt, 5)]
                for c in range(SC):
                    last = nc.tensor.matmul(p_att[0:T, :], hidT[0:CW[c], c, :], cxs[place][0:CW[c], c, :],
                                            start=(c == 0), stop=(c == SC - 1))
                    if c == SC - 1:
                        last.then_inc(s_att, 1)
                    if c < 2:
                        next(early[0], None)
                        next(early[0], None)
                    elif c < 4:
                        next(early[1], None)
                        next(early[1], None)
                    elif c == 4 and not first:
                        run(early[0], ranks(b - 1))
                run(*early)

            pe.wait_ge(s_con0, 16)
            pe.wait_ge(s_ctx_first, 16)
            for c in range(SC):
                if c == 2:
                    pe.wait_ge(s_ctx[0], 32)
                if c == 3:
                    pe.wait_ge(s_ctxD, 1)
                if c > 3:
                    pe.wait_ge(s_ctxA, c - 3)
                run(context_transposes(0, c))
            pe.wait_ge(s_xn, 1)
            transpose_rows(xn, s_xnps)
            pe.wait_ge(s_con, 48)
            batches(pe, step)
            pe.wait_ge(s_t, NB)
            transpose_rows(tn, s_tps)
            run(logits(NB - 1))
            run(ranks(NB - 1))
            pe.wait_ge(s_sum, NB + 1)
            nc.tensor.matmul(p_lg[:, 0:E], ones[0:T, :], hot_sum[:, :], start=True, stop=True
                             ).then_inc(s_cntps, 1)
            pe.wait_ge(s_blkhot, 1)
            for b in range(NB):
                for h in range(2):
                    last = nc.tensor.matmul(p_rk[BLK * h:BLK * h + BLK, 0:NCOL], row_hot[:, b, :], blk_hot[:, b, :],
                                            start=(b == 0), stop=(b == NB - 1))
            last.then_inc(s_idps, 1)

            def transpose_pair(buf, rows):
                pe.wait_ge(s_gt[buf], rows)
                for k in range(KD):
                    last = nc.tensor.transpose(p_blk[:, P * k:P * k + P], g_t[buf][:, P * k:P * k + P], ident)
                last.then_inc(s_bps, 2)

            def first_layer(slot, par, first, large):
                for k in range(KD):
                    if large:
                        for h in range(2):
                            last = nc.tensor.matmul(p_h[BLK * h:BLK * h + BLK, :],
                                                    pairT[:, k, BLK * par:BLK * par + BLK],
                                                    W1[slot][:, k, D * h:D * h + D],
                                                    start=(k == 0), stop=(k == KD - 1))
                            if first and k == 0 and h == 0:
                                last.then_inc(s_w1_used, 1)
                    else:
                        for q in range(4):
                            chunk = 4 * (q % 2) + q // 2
                            w = W1[slot][:, k, :].rearrange("p (n f) -> p n f", f=P)[:, chunk:chunk + 3:2, :]
                            last = nc.tensor.matmul(p_h[SMALL * q:SMALL * q + SMALL, 0:2 * P],
                                                    pairT[:, k, BLK * par:BLK * par + SMALL], w,
                                                    start=(k == 0), stop=(k == KD - 1),
                                                    tile_position=(0, SMALL * q))
                            if first and k == 0 and q == 0:
                                last.then_inc(s_w1_used, 1)
                last.then_inc(s_hp, 1)

            def transpose_hidden(chunks, w2_used):
                for c in range(chunks):
                    last = nc.tensor.transpose(p_hT[:, P * c:P * c + P], h_pre[:, P * c:P * c + P], ident)
                    if c == 0 and w2_used:
                        last.then_inc(s_w2_used, 1)
                last.then_inc(s_hTp, 1)

            def second_layer(j, slot):
                pe.wait_ge(s_act, j + 1)
                for c in range(KF):
                    for h in range(2):
                        last = nc.tensor.matmul(p_y[BLK * h:BLK * h + BLK, 0:HD], hT[:, 2 * (c % 4) + c // 4, :],
                                                W2[slot][:, c, HD * h:HD * h + HD],
                                                start=(c == 0), stop=(c == KF - 1))
                last.then_inc(s_y, 1)

            def unit(j, e, rnd, slot, before_slot, first):
                by_size(pe, j, lambda large: unit_of(j, rnd, slot, before_slot, first, large))

            def unit_of(j, rnd, slot, before_slot, first, large):
                pe.wait_ge(s_pairT, j + 1)
                if first:
                    for h in range(2):
                        pe.wait_ge(s_w1[slot][h], 16 * rnd + 16)
                if before_slot is not None:
                    pe.wait_ge(s_hc, j)
                if isinstance(j, int):
                    first_layer(slot, 0, first, large)
                else:
                    with pe.If(pe.snap(j % 2) > 0):
                        first_layer(slot, 1, first, large)
                        with pe.If(pe.snap(j % 4) > 1):
                            transpose_pair(0, 4 * j + 20)
                        with pe.Else():
                            transpose_pair(1, 4 * j + 12)
                    with pe.Else():
                        first_layer(slot, 0, first, large)
                if before_slot is not None:
                    second_layer(j - 1, before_slot)
                pe.wait_ge(s_hc, j + 1)
                transpose_hidden(4 if large else 2, first and before_slot is not None)
                if first:
                    for h in range(2):
                        pe.wait_ge(s_w2[slot][h], 16 * rnd + 16)

            pe.wait_ge(s_table, 1)
            pe.wait_ge(s_ids, 3)
            transpose_pair(0, 16)
            last = blocks_of_experts(pe, unit)
            second_layer(last, (E - 1) % SLOTS)

        @block.scalar
        def _(act):
            def copy_context(b, groups):
                for c in groups:
                    act.wait_ge(s_cps, SC * b + (c + 1))
                    nc.scalar.copy(ctxT[:, :, P * c:P * c + CW[c]],
                                   p_c[c % 3][:, :].rearrange("p (k f) -> p k f", k=KD)[:, :, 0:CW[c]]
                                   ).then_inc(s_ctxA, 1)

            def copy_rows(dst, wait, signal, b):
                act.wait_ge(wait, b + 1)
                nc.scalar.copy(dst[:, :, :], p_t[:, 0:KD * T].rearrange("p (k t) -> p k t", k=KD)).then_inc(signal, 1)

            def gate_tanh(b):
                act.wait_ge(s_top, b + 1)
                nc.scalar.activation(gate[:, :], top[:, :], ACT.Tanh, scale=0.5).then_inc(s_tanh, 1)

            def step(b, rnd, place, first, last_batch):
                act.wait_ge(s_x1ps, b + 1)
                nc.scalar.activation(hid[:, 0:SA], p_xa[0:T, 0:SA], ACT.Gelu_apprx_tanh).then_inc(s_gelu, 1)
                nc.scalar.activation(hid[:, SA:S], p_xb[0:T, 0:S - SA], ACT.Gelu_apprx_tanh).then_inc(s_gelu, 1)
                if not last_batch:
                    copy_context(b + 1, (1, 2))
                if not first:
                    copy_rows(tT, s_tps, s_tT, b - 1)
                if not last_batch:
                    copy_context(b + 1, (3,))
                act.wait_ge(s_hps, b + 1)
                nc.scalar.copy(hidT[:, 0:3, :], p_xa[:, 0:3 * T].rearrange("p (c t) -> p c t", c=3))
                nc.scalar.copy(hidT[:, 3:5, :], p_xb[:, 0:2 * T].rearrange("p (c t) -> p c t", c=2))
                nc.scalar.copy(hidT[0:CW[5], 5, :], p_xb[0:CW[5], 2 * T:3 * T]).then_inc(s_hidT, 1)
                if not last_batch:
                    copy_context(b + 1, (4,))
                    copy_rows(xnT, s_xnps, s_xnT, b + 1)
                    copy_context(b + 1, (5,))
                if not first:
                    gate_tanh(b - 1)

            copy_context(0, range(1, SC))
            copy_rows(xnT, s_xnps, s_xnT, 0)
            batches(act, step)
            copy_rows(tT, s_tps, s_tT, NB - 1)
            gate_tanh(NB - 1)

            def copy_pair(blocks):
                act.wait_ge(s_bps, blocks)
                nc.scalar.copy(pairT[:, :, :], p_blk[:, :].rearrange("p (k t) -> p k t", k=KD)).then_inc(s_pairT, 2)

            act.wait_ge(s_table, 1)
            n = last_block(act) + 1
            copy_pair(2)
            with act.Fori(0, n) as j:
                with act.If(act.snap(j % 2) > 0):
                    copy_pair(j + 3)
                act.wait_ge(s_hb, j + 1)
                nc.scalar.activation(hT[:, :, :], hT[:, :, :], ACT.Gelu).then_inc(s_act, 1)

        @block.vector
        def _(dve):
            def apart():
                dve.sem_inc(s_apart_v, 1)

            def norm(b, src, bn, ag, ve, rs, s_bn, s_ag, s_ve, s_rs, dst, signal):
                nc.vector.bn_stats(bn[:, :], src).then_inc(s_bn, 1)
                dve.wait_ge(s_bn, b + 1)
                apart()
                nc.vector.bn_aggr(ag[:, :], bn[:, :]).then_inc(s_ag, 1)
                dve.wait_ge(s_ag, b + 1)
                nc.vector.tensor_scalar(ve[:, :], ag[:, 1:2], EPS, None, ALU.add).then_inc(s_ve, 1)
                dve.wait_ge(s_rs, b + 1)
                nc.vector.tensor_scalar(dst, src, ag[:, 0:1], rs[:, 0:1], ALU.subtract, ALU.mult).then_inc(signal, 1)

            def norm_x(b, rnd, place):
                dve.wait_ge(s_x[place], 16 * rnd + 16)
                norm(b, xin[:, place, :], bn_x, ag_x, ve_x, rs_x, s_bnx, s_agx, s_vex, s_rsx, xn[:, :], s_xn)

            def route(b):
                dve.wait_ge(s_lgps, b + 1)
                nc.vector.tensor_reduce(top[:, :], p_lg[0:T, 0:E], AX.X, ALU.max).then_inc(s_top, 1)
                dve.wait_ge(s_top, b + 1)
                nc.vector.scalar_tensor_tensor(out=cand[:, :], in0=p_lg[0:T, 0:E], scalar=top[:, 0:1], in1=e_low,
                                               op0=ALU.is_ge, op1=ALU.mult).then_inc(s_cand, 1)
                dve.wait_ge(s_cand, b + 1)
                nc.vector.tensor_reduce(who[:, :], cand[:, :], AX.X, ALU.min).then_inc(s_who, 1)
                dve.wait_ge(s_who, b + 1)
                nc.vector.tensor_scalar(hot[:, :], e_low, who[:, 0:1], None, ALU.is_equal).then_inc(s_hot, 1)
                here = hot_all[:, bass.ds(b, 1), :].rearrange("p o e -> p (o e)")
                nc.vector.tensor_scalar(here, e_low, who[:, 0:1], None, ALU.is_equal).then_inc(s_rowhot, 1)

            def rank_and_gate(b, place):
                dve.wait_ge(s_rkps, b + 1)
                nc.vector.tensor_tensor_reduce(rank_tmp[:, :], p_rk[0:T, 0:E], hot[:, :], 1.0, 0.0,
                                               ALU.mult, ALU.add, rank[:, :]).then_inc(s_rank, 1)
                nc.vector.tensor_tensor(hot_sum[:, :], hot_sum[:, :], hot[:, :], ALU.add).then_inc(s_sum, 1)
                dve.wait_ge(s_rank, b + 1)
                nc.vector.tensor_scalar(over[:, :], thr[0:T], rank[:, 0:1], None, ALU.is_le).then_inc(s_over, 1)
                dve.wait_ge(s_over, b + 1)
                nc.vector.tensor_reduce(quot[:, :], over[:, :], AX.X, ALU.add).then_inc(s_quot, 1)
                dve.wait_ge(s_quot, b + 1)
                nc.vector.scalar_tensor_tensor(out=rest[:, :], in0=quot[:, :], scalar=-float(BLK), in1=rank[:, :],
                                               op0=ALU.mult, op1=ALU.add).then_inc(s_rest, 1)
                nc.vector.tensor_scalar(quot_all[:, bass.ds(b, 1)], quot[:, :], 1.0, None, ALU.mult)
                dve.wait_ge(s_rest, b + 1)
                here = row_hot[:, bass.ds(b, 1), :].rearrange("p o n -> p (o n)")
                nc.vector.tensor_scalar(here, rows64, rest[:, 0:1], None, ALU.is_equal).then_inc(s_rowhot, 1)
                dve.wait_ge(s_tanh, b + 1)
                nc.vector.tensor_scalar(xw[:, place, 0, HD:XW], gate[:, :], 0.5, 0.5, ALU.mult, ALU.add)
                nc.vector.tensor_scalar(xw[:, place, 1, HD:XW], gate[:, :], 0.5, 0.5, ALU.mult, ALU.add
                                        ).then_inc(s_gate, 1)

            def copy_context(b):
                dve.wait_ge(s_cps, SC * b + 1)
                nc.vector.tensor_copy(ctxT[:, :, 0:P], p_c[0][:, :].rearrange("p (k f) -> p k f", k=KD)
                                      ).then_inc(s_ctxD, 1)

            def step(b, rnd, place, first, last_batch):
                if not last_batch:
                    dve.wait_ge(s_xnps, b + 1)
                    norm_x(b + 1, rnd + (place + 1) // RING, (place + 1) % RING)
                    dve.wait_ge(s_x1ps, b + 1)
                    copy_context(b + 1)
                dve.wait_ge(s_gelu, 2 * b + 1)
                nc.vector.tensor_tensor(hid[:, 0:SA], hid[:, 0:SA], p_xa[0:T, 0:SA], ALU.mult)
                dve.wait_ge(s_gelu, 2 * b + 2)
                nc.vector.tensor_tensor(hid[:, SA:S], hid[:, SA:S], p_xb[0:T, 0:S - SA], ALU.mult).then_inc(s_hid, 1)
                if not first:
                    route(b - 1)
                    rank_and_gate(b - 1, (place - 1) % RING)
                dve.wait_ge(s_att, b + 1)
                dve.wait_ge(s_xwrow[place], 16 * rnd + 16)
                x2 = xw[:, place, :, 0:HD]
                nc.vector.tensor_tensor(x2, xin[:, place, :].rearrange("p (h d) -> p h d", h=2),
                                        p_att[0:T, :].rearrange("p (h d) -> p h d", h=2), ALU.add).then_inc(s_x2, 1)
                dve.wait_ge(s_x2, b + 1)
                dve.wait_ge(s_trow, 16 * b + 16)
                norm(b, x2, bn_t, ag_t, ve_t, rs_t, s_bnt, s_agt, s_vet, s_rst,
                     tn[:, :].rearrange("p (h d) -> p h d", h=2), s_t)

            nc.vector.memset(hot_sum[:, :], 0.0).then_inc(s_sum, 1)
            norm_x(0, 0, 0)
            copy_context(0)
            dve.wait_ge(s_con, 48)
            batches(dve, step)
            route(NB - 1)
            rank_and_gate(NB - 1, (NB - 1) % RING)

            dve.wait_ge(s_cntps, 1)
            nc.vector.tensor_tensor(cnt_over, p_lg[:, 0:E].unsqueeze(2).to_broadcast([P, E, NTHR]),
                                    thr.unsqueeze(1).to_broadcast([P, E, NTHR]), ALU.is_gt).then_inc(s_table2, 1)
            dve.wait_ge(s_table2, 1)
            nc.vector.tensor_reduce(extra[:, :], cnt_over, AX.X, ALU.add).then_inc(s_table2, 1)
            dve.wait_ge(s_table2, 2)
            nc.vector.tensor_tensor(before, extra[:, :].unsqueeze(1).to_broadcast([P, E, E]), e_before, ALU.mult
                                    ).then_inc(s_table2, 1)
            dve.wait_ge(s_table2, 3)
            nc.vector.tensor_reduce(start[:, :], before, AX.X, ALU.add).then_inc(s_table2, 1)
            dve.wait_ge(s_table2, 4)
            nc.vector.tensor_tensor(start[:, :], start[:, :], e_num, ALU.add).then_inc(s_table2, 1)
            dve.wait_ge(s_table2, 5)
            dve.wait_ge(s_rowhot, 2 * NB)
            nc.vector.tensor_tensor(start_tok, hot_all[:, :, :], start[0:T, :].unsqueeze(1).to_broadcast([T, NB, E]),
                                    ALU.mult).then_inc(s_table2, 1)
            nc.vector.scalar_tensor_tensor(out=ends[:, 0:E], in0=start[:, :], scalar=1.0, in1=extra[:, :],
                                           op0=ALU.add, op1=ALU.add)
            nc.vector.tensor_tensor(ends[:, E:E + 1], start[:, E - 1:E], extra[:, E - 1:E], ALU.add
                                    ).then_inc(s_table, 1)
            dve.wait_ge(s_table2, 6)
            nc.vector.tensor_reduce(blk_of[:, :], start_tok, AX.X, ALU.add).then_inc(s_table2, 1)
            dve.wait_ge(s_table2, 7)
            nc.vector.tensor_tensor(blk_of[:, :], blk_of[:, :], quot_all[:, :], ALU.add).then_inc(s_table2, 1)
            dve.wait_ge(s_table2, 8)
            nc.vector.tensor_tensor(blk_hot, blks.unsqueeze(1).to_broadcast([T, NB, NCOL]),
                                    blk_of[:, :].unsqueeze(2).to_broadcast([T, NB, NCOL]), ALU.is_equal
                                    ).then_inc(s_table2, 1)
            dve.wait_ge(s_table2, 9)
            nc.vector.tensor_tensor(blk_hot, blk_hot, tok_low.unsqueeze(2).to_broadcast([T, NB, NCOL]), ALU.mult
                                    ).then_inc(s_blkhot, 1)
            dve.wait_ge(s_idps, 1)
            for h in range(2):
                half = slice(BLK * h, BLK * h + BLK)
                nc.vector.tensor_scalar(id_tok[half, 0:NCOL - 1], p_rk[half, h:NCOL - 1 + h], float(TOK), None, ALU.add
                                        ).then_inc(s_ids, 1)
            nc.vector.tensor_scalar(id_half[:, :], p_rk[:, 0:NCOL], 2.0, halves, ALU.mult, ALU.add).then_inc(s_ids, 1)

            def finish(j, slot):
                dve.wait_ge(s_y, j + 1)
                nc.vector.tensor_tensor(y_b, p_y[:, 0:HD], b2s[:, slot], ALU.add).then_inc(s_yb, 1)
                odd = dve.snap(j % 2) if not isinstance(j, int) else j % 2
                xg = g_x2[:, bass.ds(odd * XW, HD)]
                gates = g_x2[:, bass.ds(odd * XW + HD, 1)]
                yo = y_out2[:, bass.ds(odd * HD, HD)]
                dve.wait_ge(s_gx, 16 * j + 16)
                dve.wait_ge(s_y_free, j + 1)
                dve.wait_ge(s_yb, j + 1)
                nc.vector.scalar_tensor_tensor(out=yo, in0=y_b, scalar=gates, in1=xg,
                                               op0=ALU.mult, op1=ALU.add).then_inc(s_yo, 1)

            def unit(j, e, rnd, slot, before_slot, first):
                by_size(dve, j, lambda large: unit_of(j, e, rnd, slot, before_slot, first, large))

            def unit_of(j, e, rnd, slot, before_slot, first, large):
                dve.wait_ge(s_hp, j + 1)
                cols = slice(0, D if large else 2 * P)
                nc.vector.tensor_copy(h_pre[:, cols], p_h[:, cols]).then_inc(s_hc, 1)
                if before_slot is not None:
                    finish(j - 1, before_slot)
                    if first:
                        dve.sem_inc(s_yb_used, 1)
                if first:
                    dve.wait_ge(s_b2[slot], 32 * rnd + 32)
                n = BLK if large else SMALL
                bias = b1s[:, bass.ds(e, 1), :].rearrange("p o c -> p (o c)").unsqueeze(2).to_broadcast([P, KF, n])
                dve.wait_ge(s_hTp, j + 1)
                nc.vector.tensor_tensor(hT[:, :, 0:n], p_hT[:, 0:KF * n].rearrange("p (c t) -> p c t", c=KF), bias,
                                        ALU.add).then_inc(s_hb, 1)

            nc.vector.memset(hT[:, :, :], 0.0).then_inc(s_hT0, 1)
            dve.wait_ge(s_hT0, 1)
            dve.wait_ge(s_table, 1)
            dve.wait_ge(s_ids, 3)
            last = blocks_of_experts(dve, unit)
            finish(last, (E - 1) % SLOTS)

        @block.gpsimd
        def _(pool):
            def apart():
                pool.sem_inc(s_apart_p, 1)

            def inverse_root(b, ve, rs, s_ve, s_rs):
                pool.wait_ge(s_ve, b + 1)
                nc.gpsimd.tensor_tensor(rs[:, :], ve[:, :], neg_half, ALU.pow).then_inc(s_rs, 1)

            def step(b, rnd, place, first, last_batch):
                if not last_batch:
                    inverse_root(b + 1, ve_x, rs_x, s_vex, s_rsx)
                inverse_root(b, ve_t, rs_t, s_vet, s_rst)

            pool.sem_inc(s_trow, 16)
            for r in range(RING):
                pool.sem_inc(s_xwrow[r], 16)
            bound_t, bound_x = pool.to_reg(TOK - 1), pool.to_reg(2 * TOK - 1)
            pool.wait_ge(s_con0, 16)
            inverse_root(0, ve_x, rs_x, s_vex, s_rsx)
            batches(pool, step)

            def column(j):
                return slice(j, j + 1) if isinstance(j, int) else bass.ds(j, 1)

            def gather_t(j, buf):
                nc.gpsimd.tensor_copy(at_t[buf][:, :], id_tok[:, column(j)]).then_inc(s_at_t, 2)
                pool.wait_ge(s_at_t, j + 2)
                apart()
                nc.gpsimd.indirect_dma_start(g_t[buf], None, t_rows,
                                             bass.IndirectOffsetOnAxis(ap=at_t[buf][:, :], axis=0),
                                             bounds_check=bound_t, oob_is_err=False).then_inc(s_gt[buf], 16)

            def gather_x(j, par):
                nc.gpsimd.tensor_copy(at_x[par][:, :], id_half[:, column(j)]).then_inc(s_at_x, 1)
                pool.wait_ge(s_at_x, j + 1)
                apart()
                nc.gpsimd.indirect_dma_start(g_x[par], None, xw_rows,
                                             bass.IndirectOffsetOnAxis(ap=at_x[par][:, :], axis=0),
                                             bounds_check=bound_x, oob_is_err=False).then_inc(s_gx, 16)

            def scatter(j, par):
                nc.gpsimd.tensor_copy(at_out[par][:, :], id_half[:, column(j)]).then_inc(s_at_out, 1)
                pool.wait_ge(s_at_out, j + 1)
                pool.wait_ge(s_yo, j + 1)
                apart()
                nc.gpsimd.indirect_dma_start(out_halves, bass.IndirectOffsetOnAxis(ap=at_out[par][:, :], axis=0),
                                             y_out[par], None, bounds_check=bound_x, oob_is_err=False
                                             ).then_inc(s_done[par], 16)

            pool.wait_ge(s_att, NB)
            for g in (*g_t, g_x2):
                nc.gpsimd.memset(g, 0.0).then_inc(s_g0, 1)
            pool.wait_ge(s_trow, 16 * NB + 16)
            pool.wait_ge(s_ids, 3)
            pool.wait_ge(s_g0, 3)
            gather_t(0, 0)
            gather_t(2, 1)
            for r in range(RING):
                pool.wait_ge(s_xwrow[r], 16 * (1 + len(range(r, NB, RING))))
            gather_x(0, 0)
            last = last_block(pool)

            def fetch_pair(j, buf):
                pool.wait_ge(s_bps, j + 2)
                apart()
                gather_t(j + 4, buf)

            def block_step(j, par):
                if isinstance(j, int):
                    if par == 0:
                        fetch_pair(j, 0)
                    if j > 0:
                        scatter(j - 1, 1 - par)
                else:
                    if par == 0:
                        with pool.If(pool.snap(j % 4) > 1):
                            fetch_pair(j, 1)
                        with pool.Else():
                            fetch_pair(j, 0)
                    scatter(j - 1, 1 - par)
                pool.wait_ge(s_gx, 16 * j + 16)
                apart()
                gather_x(j + 1, 1 - par)
                if not isinstance(j, int):
                    pool.wait_ge(s_done[par], 8 * (j - par))
                pool.sem_inc(s_y_free, 1)

            block_step(0, 0)
            block_step(1, 1)
            with pool.Fori(2, last + 1) as j:
                by_parity(pool, j, lambda par: block_step(j, par))
            by_parity(pool, last, lambda par: scatter(last, par))

            pool.wait_ge(s_gx, 16 * last + 32)
            apart()
            with pool.If(pool.snap(last % 2) > 0):
                pool.wait_ge(s_done[0], 8 * last + 8)
                pool.wait_ge(s_done[1], 8 * last + 8)
                pool.sem_inc(s_apart_p, 1)
                with pool.If(pool.snap(last % 4) > 1):
                    pool.wait_ge(s_gt[0], 4 * last + 20)
                    pool.wait_ge(s_gt[1], 4 * last + 20)
                    pool.sem_inc(s_apart_p, 1)
                with pool.Else():
                    pool.wait_ge(s_gt[0], 4 * last + 28)
                    pool.wait_ge(s_gt[1], 4 * last + 12)
                    pool.sem_inc(s_apart_p, 1)
            with pool.Else():
                pool.wait_ge(s_done[0], 8 * last + 16)
                pool.wait_ge(s_done[1], 8 * last)
                pool.sem_inc(s_apart_p, 1)
                with pool.If(pool.snap(last % 4) > 1):
                    pool.wait_ge(s_gt[0], 4 * last + 24)
                    pool.wait_ge(s_gt[1], 4 * last + 24)
                    pool.sem_inc(s_apart_p, 1)
                with pool.Else():
                    pool.wait_ge(s_gt[0], 4 * last + 32)
                    pool.wait_ge(s_gt[1], 4 * last + 16)
                    pool.sem_inc(s_apart_p, 1)


def kernel(x, ctx_1024, L0_ffn_router_w, L0_ffn_w1, L0_ffn_b1, L0_ffn_w2, L0_ffn_b2):
    import concourse.bacc as bacc
    from concourse.bass_utils import run_bass_kernel_spmd

    def laid(a, shape, order):
        return np.ascontiguousarray(np.transpose(np.reshape(np.asarray(a), shape), order))

    ctx = np.asarray(ctx_1024)
    full = P * (SC - 1)
    arrays = {
        "x": np.ascontiguousarray(x),
        "ctx_main": laid(ctx[:, 0:full], (NB, SC - 1, P, D), (0, 2, 1, 3)),
        "ctx_rest": np.ascontiguousarray(ctx[:, full:S]),
        "router": laid(L0_ffn_router_w, (KD, P, E), (1, 0, 2)),
        "w1": laid(L0_ffn_w1, (E, KD, P, F), (0, 2, 1, 3)),
        "b1": laid(L0_ffn_b1, (E, 2, 4, P), (3, 0, 2, 1)).reshape(P, E, KF),
        "w2": laid(L0_ffn_w2, (E, KF, P, D), (0, 2, 1, 3)),
        "b2": np.ascontiguousarray(L0_ffn_b2).reshape(E, 2, HD),
        "consts": shape_constants(),
    }
    nc = bacc.Bacc("TRN2", target_bir_lowering=False, num_devices=1)
    args = [nc.dram_tensor(f"in_{n}", a.shape, mybir.dt.from_np(a.dtype), kind="ExternalInput").ap()
            for n, a in arrays.items()]
    out = nc.dram_tensor("out", (NB, T, D), F32, kind="ExternalOutput").ap()
    build(nc, *args, out)
    r = run_bass_kernel_spmd(nc, [{f"in_{n}": a for n, a in arrays.items()}], core_ids=[0])
    return r.results[0]["out"]
```

```python
from contextlib import ExitStack

import numpy as np

import concourse.bass as bass
from concourse import mybir

F32 = mybir.dt.float32
I32 = mybir.dt.int32
U32 = mybir.dt.uint32
ALU = mybir.AluOpType
ACT = mybir.ActivationFunctionType
AX = mybir.AxisListType

P = 128
NB, T, D, S = 8, 100, 512, 722
E, F = 16, 1024
TOK = NB * T
KD = D // P
KF = F // P
SC = -(-S // P)
CW = [min(P, S - P * c) for c in range(SC)]
SA = 3 * P
BLK = 64
SMALL = 32
MAXB = E - 1 + -(-(TOK - E + 1) // BLK)
NCOL = MAXB + 6
NTHR = TOK // BLK
SLOTS = 5
RING = 3
HD = D // 2
XW = HD + 1
EPS = 1e-5
EARLY = (0, 1, 1, 1, 1, 1, 2, 3)

C_ID, C_NH, C_ONE = 0, P, P + 1
C_TRI = C_ONE + P
C_EM = C_TRI + T
C_THR = C_EM + E
C_PM = C_THR + NTHR
C_BLK = C_PM + BLK
C_TOK = C_BLK + NCOL
C_LT = C_TOK + NB
C_E = C_LT + E * E
C_HALF = C_E + E
C_ALL = C_HALF + 1


def shape_constants():
    c = np.zeros((P, C_ALL), np.float32)
    p = np.arange(P)
    c[:, C_ID:C_ID + P] = np.eye(P)
    c[:, C_ONE:C_ONE + P] = 1
    c[:, C_TRI:C_TRI + T] = p[:, None] < np.arange(T)
    c[:, C_EM:C_EM + E] = np.arange(E) - E
    c[:, C_THR:C_THR + NTHR] = BLK * (1 + np.arange(NTHR))
    c[:, C_PM:C_PM + BLK] = np.arange(BLK)
    c[:, C_BLK:C_BLK + NCOL] = np.arange(NCOL)
    c[:, C_TOK:C_TOK + NB] = p[:, None] + T * np.arange(NB) - TOK
    c[:, C_LT:C_LT + E * E] = (np.arange(E)[:, None] > np.arange(E)).ravel()
    c[:, C_E:C_E + E] = np.arange(E)
    c[:, C_HALF] = 2 * TOK + p // BLK
    c[:, C_NH] = -0.5
    return c


def build(nc, x, ctx_main, ctx_rest, ctxT_a, ctxT_b, router, w1, b1, w2, b2, consts, out):
    t_rows = nc.dram_tensor("t_rows", (TOK, D), F32).ap()
    xw_rows = nc.dram_tensor("xw_rows", (2 * TOK, XW), F32).ap()
    xw_by_token = xw_rows.rearrange("(n h) d -> n h d", h=2)
    out_halves = out.rearrange("b t (h d) -> (b t h) d", h=2)

    with ExitStack() as stack:
        def sb(name, shape, dt=F32):
            return stack.enter_context(nc.sbuf_tensor(name, shape, dt))

        def sem(name):
            return stack.enter_context(nc.semaphore(name))

        def sems(name, n):
            return [sem(f"{name}{i}") for i in range(n)]

        W1_early = sb("W1_early", [P, SLOTS - 1, KD, F])
        W2_early = sb("W2_early", [P, SLOTS - 1, KF, D])
        con = sb("con", [P, C_ALL])
        rw = sb("rw", [P, KD, E])
        b1s = sb("b1s", [P, E, KF])
        work = sb("work", [P, RING * SC * D])
        area = sb("area", [P, KD * S + RING * D])
        ctxTs = [area[:, KD * lo:KD * hi].rearrange("p (k s) -> p k s", k=KD) for lo, hi in ((0, SA), (SA, S))]
        xin = area[0:T, KD * S:KD * S + RING * D].rearrange("p (r d) -> p r d", r=RING)
        xn = sb("xn", [T, D])
        xnT = sb("xnT", [P, KD, T])
        hid = sb("hid", [T, S])
        hidT = sb("hidT", [P, SC, T])
        xw = sb("xw", [T, RING, 2, XW])
        tn = sb("tn", [T, D])
        tT = sb("tT", [P, KD, T])
        bn_x, ag_x, ve_x, rs_x = sb("bn_x", [T, 6]), sb("ag_x", [T, 2]), sb("ve_x", [T, 1]), sb("rs_x", [T, 1])
        bn_t, ag_t, ve_t, rs_t = sb("bn_t", [T, 6]), sb("ag_t", [T, 2]), sb("ve_t", [T, 1]), sb("rs_t", [T, 1])
        top, cand, who, gate = sb("top", [T, 1]), sb("cand", [T, E]), sb("who", [T, 1]), sb("gate", [T, 1])
        hot, hot_sum, hot_all = sb("hot", [T, E]), sb("hot_sum", [T, E]), sb("hot_all", [T, NB, E])
        rank_tmp, rank, over = sb("rank_tmp", [T, E]), sb("rank", [T, 1]), sb("over", [T, NTHR])
        quot, quot_all, rest = sb("quot", [T, 1]), sb("quot_all", [T, NB]), sb("rest", [T, 1])
        row_hot = sb("row_hot", [T, NB, BLK])
        cnt_over = ctxTs[0][:, 0, 0:E * NTHR].rearrange("p (e n) -> p e n", e=E)
        before_of = ctxTs[0][:, 1, 0:E * E].rearrange("p (e n) -> p e n", e=E)
        start_tok = ctxTs[0][0:T, 2, 0:NB * E].rearrange("p (b e) -> p b e", b=NB)
        blk_hot = ctxTs[0][0:T, 3, 0:NB * NCOL].rearrange("p (b n) -> p b n", b=NB)
        extra, start, blk_of = sb("extra", [P, E]), sb("start", [P, E]), sb("blk_of", [T, NB])
        ends = sb("ends", [P, E + 1], I32)
        id_tok, id_half = sb("id_tok", [P, NCOL], U32), sb("id_half", [P, NCOL], U32)
        at_t, at_x, at_out = ([sb(f"{n}{i}", [P, 1], U32) for i in range(2)] for n in ("at_t", "at_x", "at_out"))

        cxs = [work[:, SC * D * i:SC * D * (i + 1)].rearrange("p (c d) -> p c d", c=SC) for i in range(RING)]
        used = [0]

        def part2(n):
            used[0] += n
            assert used[0] <= RING * SC * D
            return work[:, used[0] - n:used[0]]
        g_t = [part2(D) for _ in range(2)]
        g_x2 = part2(2 * XW)
        g_x = [g_x2[:, XW * i:XW * i + XW] for i in range(2)]
        pairT = part2(KD * P).rearrange("p (k t) -> p k t", k=KD)
        h_pre = part2(D)
        hT = part2(KF * BLK).rearrange("p (c t) -> p c t", c=KF)
        y_out2 = part2(2 * HD)
        y_out = [y_out2[:, HD * i:HD * i + HD] for i in range(2)]
        b2s = [part2(D)[0:1], part2(D)[0:1], hid[0:1, 0:D], xn[0:1, :],
               hidT[:, :, :].rearrange("p c t -> p (c t)")[0:1, 0:D]]
        assert len(b2s) == SLOTS
        W1 = [W1_early[:, s] for s in range(SLOTS - 1)] + [part2(KD * F).rearrange("p (k f) -> p k f", k=KD)]
        W2 = ([W2_early[:, s] for s in range(SLOTS - 1)]
              + [area[:, 0:KF * D].rearrange("p (k d) -> p k d", k=KF)])

        ident, ones = con[:, C_ID:C_ID + P], con[:, C_ONE:C_ONE + P]
        tri, e_low = con[0:T, C_TRI:C_TRI + T], con[0:T, C_EM:C_EM + E]
        thr = con[:, C_THR:C_THR + NTHR]
        rows64, blks = con[0:T, C_PM:C_PM + BLK], con[0:T, C_BLK:C_BLK + NCOL]
        tok_low = con[0:T, C_TOK:C_TOK + NB]
        e_before = con[:, C_LT:C_LT + E * E].rearrange("p (e n) -> p e n", e=E)
        e_num, halves, neg_half = con[:, C_E:C_E + E], con[:, C_HALF:C_HALF + 1], con[0:T, C_NH:C_NH + 1]

        bank = [stack.enter_context(nc.psum_tensor(f"bank{i}", [P, 512], F32)) for i in range(8)]
        p_xa, p_xb, p_t, p_ha, p_hb, p_xn, p_att, p_lg = bank
        p_rk = p_lg[:, 64:128]
        p_h, p_hT, p_blk, p_y = bank[0], bank[1], bank[2], bank[5]

        s_con0, s_con, s_ctxT = sem("s_con0"), sem("s_con"), sems("s_ctxT", 2)
        s_x, s_ctx = sems("s_x_in", RING), sems("s_ctx", RING)
        s_w1, s_w2 = ([sems(f"{n}_{i}_", 2) for i in range(SLOTS)] for n in ("s_w1", "s_w2"))
        s_b2 = sems("s_b2", SLOTS)
        s_trow, s_xwrow = sem("s_trow"), sems("s_xwrow", RING)
        s_x1ps, s_tps, s_lgps = sems("s_x1ps", 2), sem("s_tps"), sem("s_lgps")
        s_hps, s_xnps, s_att, s_rkps = sems("s_hps", 2), sem("s_xnps"), sem("s_att"), sem("s_rkps")
        s_cntps, s_idps = sem("s_cntps"), sem("s_idps")
        s_gelu, s_tT, s_hidT = sems("s_gelu", 2), sem("s_tT"), sems("s_hidT", 2)
        s_tanh, s_xnT = sem("s_tanh"), sem("s_xnT")
        s_bnx, s_agx, s_vex, s_rsx, s_xn = (sem(n) for n in ("s_bnx", "s_agx", "s_vex", "s_rsx", "s_xn"))
        s_bnt, s_agt, s_vet, s_rst, s_t = (sem(n) for n in ("s_bnt", "s_agt", "s_vet", "s_rst", "s_t"))
        s_hid = sems("s_hid", 2)
        s_x2, s_top, s_cand, s_who, s_hot = (
            sem(n) for n in ("s_x2", "s_top", "s_cand", "s_who", "s_hot"))
        s_sum, s_rank, s_over, s_quot, s_rest, s_rowhot, s_gate = (
            sem(n) for n in ("s_sum", "s_rank", "s_over", "s_quot", "s_rest", "s_rowhot", "s_gate"))
        s_table, s_blkhot, s_ids, s_g0 = sem("s_table"), sem("s_blkhot"), sem("s_ids"), sem("s_g0")
        s_table2, s_y_free = sem("s_table2"), sem("s_y_free")
        s_hT0 = sem("s_hT0")
        s_apart_v, s_apart_p = sem("s_apart_v"), sem("s_apart_p")
        s_bps, s_hp, s_hTp, s_y = sem("s_bps"), sem("s_hp"), sem("s_hTp"), sem("s_y")
        s_w1_used, s_w2_used = sem("s_w1_used"), sem("s_w2_used")
        s_pairT, s_act = sem("s_pairT"), sem("s_act")
        s_hc, s_hb, s_yo = sem("s_hc"), sem("s_hb"), sem("s_yo")
        s_at_t, s_at_x, s_at_out = sem("s_at_t"), sem("s_at_x"), sem("s_at_out")
        s_gt, s_gx, s_done = sems("s_gt", 2), sem("s_gx"), sems("s_done", 2)

        block = stack.enter_context(nc.Block())

        def batches(eng, step, done=0):
            if not done:
                step(0, 0, 0, True, False)
            with eng.Fori(0, (NB - 2) // RING) as i:
                for u in range(RING):
                    step(RING * i + (1 + u), i + (1 + u) // RING, (1 + u) % RING, False, False)
            step(NB - 1, (NB - 1) // RING, (NB - 1) % RING, False, True)

        def by_parity(eng, j, step):
            with eng.If(eng.snap(j % 2) > 0):
                step(1)
            with eng.Else():
                step(0)

        def by_size(eng, j, body):
            at = slice(j, j + 1) if isinstance(j, int) else bass.ds(j, 1)
            row = eng.value_load(id_half[SMALL:SMALL + 1, at], min_val=0, max_val=2 * TOK)
            with eng.If(row < 2 * TOK):
                body(True)
            with eng.Else():
                body(False)

        def last_block(eng):
            return eng.value_load(ends[0:1, E:E + 1], min_val=E - 1, max_val=MAXB - 1)

        def blocks_of_experts(eng, unit):
            def rest_of(e, rnd, slot, first, end):
                with eng.If(end > first + 1):
                    with eng.Fori(first + 1, end) as j:
                        unit(j, e, rnd, slot, (slot, rnd), False)

            end = eng.value_load(ends[0:1, 0:1], min_val=1, max_val=MAXB - E + 1)
            unit(0, 0, 0, 0, None, True)
            rest_of(0, 0, 0, 0, end)
            with eng.Fori(0, (E - 1) // SLOTS) as g:
                first = eng.value_load(ends[0:1, bass.ds(SLOTS * g, 1)], min_val=1, max_val=MAXB - 1)
                for s in range(SLOTS):
                    e, rnd, slot = SLOTS * g + (1 + s), g + (1 + s) // SLOTS, (1 + s) % SLOTS
                    end = eng.value_load(ends[0:1, bass.ds(e, 1)], min_val=2, max_val=MAXB)
                    unit(first, e, rnd, slot, (s, g), True)
                    rest_of(e, rnd, slot, first, end)
                    first = end
            assert (E - 1) % SLOTS == 0
            return last_block(eng)

        @block.sync
        def _(sp):
            def load_x(b):
                sp.dma_start(xin[:, b % RING, :], x[b]).then_inc(s_x[b % RING], 16)

            def load_ctx(b):
                r = b % RING
                sp.dma_start(cxs[r][:, 0:SC - 1, :], ctx_main[b]).then_inc(s_ctx[r], 16)
                sp.dma_start(cxs[r][0:CW[-1], SC - 1, :], ctx_rest[b]).then_inc(s_ctx[r], 16)

            def load_half(dst, src, signals, h):
                n = dst.shape[1] // 2
                sp.dma_start(dst[:, n * h:n * h + n], src[:, n * h:n * h + n]).then_inc(signals[h], 16)

            def load_layer(dst, src, signals):
                for h in range(2):
                    load_half(dst, src, signals, h)

            def load_ctxT(b, part):
                sp.dma_start(ctxTs[part], (ctxT_a, ctxT_b)[part][b]).then_inc(s_ctxT[part], 16)

            sp.dma_start(con[:, 0:C_ONE], consts[:, 0:C_ONE]).then_inc(s_con0, 16)
            sp.dma_start(xin[:, 0, :], x[0]).then_inc(s_x[0], 16)
            load_ctxT(0, 0)
            load_ctxT(0, 1)
            load_ctx(0)
            sp.dma_start(con[:, C_ONE:C_ALL], consts[:, C_ONE:C_ALL]).then_inc(s_con, 16)
            sp.dma_start(rw[:, :, :], router).then_inc(s_con, 16)
            sp.dma_start(b1s[:, :, :], b1).then_inc(s_con, 16)
            load_x(1)
            early_weights = iter([(W[e], w[e], signal[e], h) for e in range(SLOTS - 1)
                                  for W, w, signal in ((W1, w1, s_w1), (W2, w2, s_w2)) for h in range(2)])

            def load_weights(n):
                for _ in range(n):
                    load_half(*next(early_weights))

            for b in range(NB):
                if b + 1 < NB:
                    for part in range(2):
                        sp.wait_ge(s_x1ps[part], b + 1)
                        load_ctxT(b + 1, part)
                if b > 0:
                    sp.wait_ge(s_t, b)
                    sp.dma_start(t_rows[T * (b - 1):T * b, :], tn[:, :]).then_inc(s_trow, 16)
                if b == 0:
                    load_ctx(1)
                    load_x(2)
                    load_ctx(2)
                elif b + 2 < NB:
                    sp.wait_ge(s_att, b)
                    sp.wait_ge(s_x2, b)
                    load_x(b + 2)
                    load_ctx(b + 2)
                load_weights(EARLY[b])
                if b > 0:
                    sp.wait_ge(s_gate, b)
                    sp.dma_start(xw_by_token[T * (b - 1):T * b], xw[:, (b - 1) % RING]
                                 ).then_inc(s_xwrow[(b - 1) % RING], 16)
            sp.wait_ge(s_att, NB)
            load_weights(2)
            sp.wait_ge(s_t, NB)
            sp.dma_start(t_rows[T * (NB - 1):TOK, :], tn[:, :]).then_inc(s_trow, 16)
            load_weights(1)
            for s in range(SLOTS):
                sp.dma_start(b2s[s], b2[s:s + 1]).then_inc(s_b2[s], 16)
            sp.wait_ge(s_gate, NB)
            sp.dma_start(xw_by_token[T * (NB - 1):TOK], xw[:, (NB - 1) % RING]).then_inc(s_xwrow[(NB - 1) % RING], 16)
            load_weights(1)
            sp.wait_ge(s_x2, NB)
            sp.wait_ge(s_idps, 1)
            sp.wait_ge(s_bps, 1)
            load_weights(4 * (SLOTS - 1) - sum(EARLY) - 4)
            load_layer(W1[SLOTS - 1], w1[SLOTS - 1], s_w1[SLOTS - 1])
            load_layer(W2[SLOTS - 1], w2[SLOTS - 1], s_w2[SLOTS - 1])

            def load_expert(e, rnd, s):
                one = slice(e, e + 1) if isinstance(e, int) else bass.ds(e, 1)
                first, second = (w[one].rearrange("o p k f -> (o p) k f") for w in (w1, w2))
                before = (s - 1) % SLOTS
                in_before = 16 * (rnd + (s - 1) // SLOTS) + 16
                sp.wait_ge(s_w1_used, e - (SLOTS - 2))
                sp.wait_ge(s_w2[before][0], in_before)
                load_half(W1[s], first, s_w1[s], 0)
                sp.wait_ge(s_w2[before][1], in_before)
                load_half(W1[s], first, s_w1[s], 1)
                sp.wait_ge(s_w2_used, e - (SLOTS - 1))
                sp.dma_start(b2s[s], b2[one]).then_inc(s_b2[s], 16)
                sp.wait_ge(s_w1[s][0], 16 * rnd + 16)
                load_half(W2[s], second, s_w2[s], 0)
                sp.wait_ge(s_w1[s][1], 16 * rnd + 16)
                load_half(W2[s], second, s_w2[s], 1)

            with sp.Fori(1, E // SLOTS) as g:
                for s in range(SLOTS):
                    load_expert(SLOTS * g + s, g, s)
            assert E % SLOTS == 1
            load_expert(E - 1, E // SLOTS, 0)

        @block.tensor
        def _(pe):
            def transpose_rows(src, dst, signal):
                for k in range(KD):
                    last = nc.tensor.transpose(dst[:, T * k:T * k + T], src[:, P * k:P * k + P], ident[0:T, 0:T])
                last.then_inc(signal, 1)

            def x1_products(part, ks):
                lo, hi = ((0, SA), (SA, S))[part]
                for k in ks:
                    last = nc.tensor.matmul((p_xa, p_xb)[part][0:T, 0:hi - lo], xnT[:, k, :], ctxTs[part][:, k, :],
                                            start=(k == 0), stop=(k == KD - 1))
                    if k == KD - 1:
                        last.then_inc(s_x1ps[part], 1)

            def transpose_hidden_part(b, part):
                pe.wait_ge(s_hid[part], b + 1)
                for c in range(3 * part, 3 * part + 3):
                    last = nc.tensor.transpose((p_ha, p_hb)[part][0:CW[c], T * (c % 3):T * (c % 3) + T],
                                               hid[:, P * c:P * c + CW[c]], ident[0:T, 0:T])
                last.then_inc(s_hps[part], 1)

            def logits(b):
                pe.wait_ge(s_tT, b + 1)
                for k in range(KD):
                    last = nc.tensor.matmul(p_lg[0:T, 0:E], tT[:, k, :], rw[:, k, :],
                                            start=(k == 0), stop=(k == KD - 1))
                last.then_inc(s_lgps, 1)

            def ranks(b):
                pe.wait_ge(s_hot, b + 1)
                pe.wait_ge(s_sum, b + 1)
                nc.tensor.matmul(p_rk[0:T, 0:E], tri, hot[:, :], start=True, stop=False)
                nc.tensor.matmul(p_rk[0:T, 0:E], ones[0:T, 0:T], hot_sum[:, :],
                                 start=False, stop=True).then_inc(s_rkps, 1)

            def attention(place, cs):
                for c in cs:
                    last = nc.tensor.matmul(p_att[0:T, :], hidT[0:CW[c], c, :], cxs[place][0:CW[c], c, :],
                                            start=(c == 0), stop=(c == SC - 1))
                    if c == SC - 1:
                        last.then_inc(s_att, 1)

            def step(b, rnd, place, first, last_batch):
                pe.wait_ge(s_ctxT[0], 16 * b + 16)
                pe.wait_ge(s_xnT, b + 1)
                x1_products(0, range(KD))
                pe.wait_ge(s_ctxT[1], 16 * b + 16)
                x1_products(1, range(KD - 1))
                transpose_hidden_part(b, 0)
                x1_products(1, [KD - 1])
                if not first:
                    pe.wait_ge(s_t, b)
                    transpose_rows(tn, p_t, s_tps)
                pe.wait_ge(s_hidT[0], b + 1)
                pe.wait_ge(s_ctx[place], 32 * rnd + 32)
                attention(place, range(3))
                transpose_hidden_part(b, 1)
                if not first:
                    logits(b - 1)
                pe.wait_ge(s_hidT[1], b + 1)
                attention(place, [3])
                if not last_batch:
                    pe.wait_ge(s_xn, b + 2)
                    transpose_rows(xn, p_xn, s_xnps)
                attention(place, [4])
                if not first:
                    ranks(b - 1)
                attention(place, [5])

            pe.wait_ge(s_con0, 16)
            pe.wait_ge(s_xn, 1)
            transpose_rows(xn, p_xn, s_xnps)
            step(0, 0, 0, True, False)
            pe.wait_ge(s_con, 48)
            batches(pe, step, 1)
            pe.wait_ge(s_t, NB)
            transpose_rows(tn, p_t, s_tps)
            logits(NB - 1)
            ranks(NB - 1)
            pe.wait_ge(s_sum, NB + 1)
            nc.tensor.matmul(p_lg[:, 0:E], ones[0:T, :], hot_sum[:, :], start=True, stop=True
                             ).then_inc(s_cntps, 1)
            pe.wait_ge(s_blkhot, 1)
            for b in range(NB):
                for h in range(2):
                    last = nc.tensor.matmul(p_rk[BLK * h:BLK * h + BLK, 0:NCOL], row_hot[:, b, :], blk_hot[:, b, :],
                                            start=(b == 0), stop=(b == NB - 1))
            last.then_inc(s_idps, 1)

            def transpose_pair(buf, rows):
                pe.wait_ge(s_gt[buf], rows)
                for k in range(KD):
                    last = nc.tensor.transpose(p_blk[:, P * k:P * k + P], g_t[buf][:, P * k:P * k + P], ident)
                last.then_inc(s_bps, 2)

            def first_layer(slot, rnd, par, first, large):
                for k in range(KD):
                    if first and k % 2 == 0:
                        pe.wait_ge(s_w1[slot][k // 2], 16 * rnd + 16)
                    if large:
                        for h in range(2):
                            last = nc.tensor.matmul(p_h[BLK * h:BLK * h + BLK, :],
                                                    pairT[:, k, BLK * par:BLK * par + BLK],
                                                    W1[slot][:, k, D * h:D * h + D],
                                                    start=(k == 0), stop=(k == KD - 1))
                            if first and k == 0 and h == 0:
                                last.then_inc(s_w1_used, 1)
                    else:
                        for q in range(4):
                            chunk = 4 * (q % 2) + q // 2
                            w = W1[slot][:, k, :].rearrange("p (n f) -> p n f", f=P)[:, chunk:chunk + 3:2, :]
                            last = nc.tensor.matmul(p_h[SMALL * q:SMALL * q + SMALL, 0:2 * P],
                                                    pairT[:, k, BLK * par:BLK * par + SMALL], w,
                                                    start=(k == 0), stop=(k == KD - 1),
                                                    tile_position=(0, SMALL * q))
                            if first and k == 0 and q == 0:
                                last.then_inc(s_w1_used, 1)
                last.then_inc(s_hp, 1)

            def transpose_hidden(chunks, w2_used):
                for c in range(chunks):
                    last = nc.tensor.transpose(p_hT[:, P * c:P * c + P], h_pre[:, P * c:P * c + P], ident)
                    if c == 0 and w2_used:
                        last.then_inc(s_w2_used, 1)
                last.then_inc(s_hTp, 1)

            def second_layer(j, slot, rnd):
                pe.wait_ge(s_yo, j + 1)
                pe.wait_ge(s_b2[slot], 16 * rnd + 16)
                for h in range(2):
                    nc.tensor.matmul(p_y[BLK * h:BLK * h + BLK, 0:HD], ones[0:1, 0:BLK],
                                     b2s[slot][:, HD * h:HD * h + HD], start=True, stop=False)
                pe.wait_ge(s_act, j + 1)
                for c in range(KF):
                    if c % (KF // 2) == 0:
                        pe.wait_ge(s_w2[slot][c // (KF // 2)], 16 * rnd + 16)
                    for h in range(2):
                        last = nc.tensor.matmul(p_y[BLK * h:BLK * h + BLK, 0:HD], hT[:, 2 * (c % 4) + c // 4, :],
                                                W2[slot][:, c, HD * h:HD * h + HD],
                                                start=False, stop=(c == KF - 1))
                last.then_inc(s_y, 1)

            def unit(j, e, rnd, slot, before, first):
                by_size(pe, j, lambda large: unit_of(j, rnd, slot, before, first, large))

            def unit_of(j, rnd, slot, before, first, large):
                pe.wait_ge(s_pairT, j + 1)
                if before is not None:
                    pe.wait_ge(s_hc, j)
                if isinstance(j, int):
                    first_layer(slot, rnd, 0, first, large)
                else:
                    with pe.If(pe.snap(j % 2) > 0):
                        first_layer(slot, rnd, 1, first, large)
                        with pe.If(pe.snap(j % 4) > 1):
                            transpose_pair(0, 4 * j + 20)
                        with pe.Else():
                            transpose_pair(1, 4 * j + 12)
                    with pe.Else():
                        first_layer(slot, rnd, 0, first, large)
                if before is not None:
                    second_layer(j - 1, *before)
                pe.wait_ge(s_hc, j + 1)
                transpose_hidden(4 if large else 2, first and before is not None)

            pe.wait_ge(s_table, 1)
            pe.wait_ge(s_ids, 3)
            transpose_pair(0, 16)
            last = blocks_of_experts(pe, unit)
            second_layer(last, (E - 1) % SLOTS, (E - 1) // SLOTS)

        @block.scalar
        def _(act):
            def copy_rows(src, dst, wait, signal, b):
                act.wait_ge(wait, b + 1)
                nc.scalar.copy(dst[:, :, :], src[:, 0:KD * T].rearrange("p (k t) -> p k t", k=KD)).then_inc(signal, 1)

            def gelu(b, part):
                lo, hi = ((0, SA), (SA, S))[part]
                act.wait_ge(s_x1ps[part], b + 1)
                nc.scalar.activation(hid[:, lo:hi], (p_xa, p_xb)[part][0:T, 0:hi - lo], ACT.Gelu_apprx_tanh
                                     ).then_inc(s_gelu[part], 1)

            def gate_tanh(b):
                act.wait_ge(s_top, b + 1)
                nc.scalar.activation(gate[:, :], top[:, :], ACT.Tanh, scale=0.5).then_inc(s_tanh, 1)

            def step(b, rnd, place, first, last_batch):
                gelu(b, 0)
                act.wait_ge(s_hps[0], b + 1)
                nc.scalar.copy(hidT[:, 0:3, :], p_ha[:, 0:3 * T].rearrange("p (c t) -> p c t", c=3)
                               ).then_inc(s_hidT[0], 1)
                gelu(b, 1)
                if not first:
                    copy_rows(p_t, tT, s_tps, s_tT, b - 1)
                act.wait_ge(s_hps[1], b + 1)
                nc.scalar.copy(hidT[:, 3:5, :], p_hb[:, 0:2 * T].rearrange("p (c t) -> p c t", c=2))
                nc.scalar.copy(hidT[0:CW[5], 5, :], p_hb[0:CW[5], 2 * T:3 * T]).then_inc(s_hidT[1], 1)
                if not last_batch:
                    copy_rows(p_xn, xnT, s_xnps, s_xnT, b + 1)
                if not first:
                    gate_tanh(b - 1)

            copy_rows(p_xn, xnT, s_xnps, s_xnT, 0)
            batches(act, step)
            copy_rows(p_t, tT, s_tps, s_tT, NB - 1)
            gate_tanh(NB - 1)

            def copy_pair(blocks):
                act.wait_ge(s_bps, blocks)
                nc.scalar.copy(pairT[:, :, :], p_blk[:, :].rearrange("p (k t) -> p k t", k=KD)).then_inc(s_pairT, 2)

            act.wait_ge(s_table, 1)
            n = last_block(act) + 1
            copy_pair(2)
            with act.Fori(0, n) as j:
                with act.If(act.snap(j % 2) > 0):
                    copy_pair(j + 3)
                act.wait_ge(s_hb, j + 1)
                nc.scalar.activation(hT[:, :, :], hT[:, :, :], ACT.Gelu).then_inc(s_act, 1)

        @block.vector
        def _(dve):
            def apart():
                dve.sem_inc(s_apart_v, 1)

            def norm(b, src, bn, ag, ve, rs, s_bn, s_ag, s_ve, s_rs, dst, signal):
                nc.vector.bn_stats(bn[:, :], src).then_inc(s_bn, 1)
                dve.wait_ge(s_bn, b + 1)
                apart()
                nc.vector.bn_aggr(ag[:, :], bn[:, :]).then_inc(s_ag, 1)
                dve.wait_ge(s_ag, b + 1)
                nc.vector.tensor_scalar(ve[:, :], ag[:, 1:2], EPS, None, ALU.add).then_inc(s_ve, 1)
                dve.wait_ge(s_rs, b + 1)
                nc.vector.tensor_scalar(dst, src, ag[:, 0:1], rs[:, 0:1], ALU.subtract, ALU.mult).then_inc(signal, 1)

            def norm_x(b, rnd, place):
                dve.wait_ge(s_x[place], 16 * rnd + 16)
                norm(b, xin[:, place, :], bn_x, ag_x, ve_x, rs_x, s_bnx, s_agx, s_vex, s_rsx, xn[:, :], s_xn)

            def route(b):
                dve.wait_ge(s_lgps, b + 1)
                nc.vector.tensor_reduce(top[:, :], p_lg[0:T, 0:E], AX.X, ALU.max).then_inc(s_top, 1)
                dve.wait_ge(s_top, b + 1)
                nc.vector.scalar_tensor_tensor(out=cand[:, :], in0=p_lg[0:T, 0:E], scalar=top[:, 0:1], in1=e_low,
                                               op0=ALU.is_ge, op1=ALU.mult).then_inc(s_cand, 1)
                dve.wait_ge(s_cand, b + 1)
                nc.vector.tensor_reduce(who[:, :], cand[:, :], AX.X, ALU.min).then_inc(s_who, 1)
                dve.wait_ge(s_who, b + 1)
                nc.vector.tensor_scalar(hot[:, :], e_low, who[:, 0:1], None, ALU.is_equal).then_inc(s_hot, 1)
                here = hot_all[:, bass.ds(b, 1), :].rearrange("p o e -> p (o e)")
                nc.vector.tensor_scalar(here, e_low, who[:, 0:1], None, ALU.is_equal).then_inc(s_rowhot, 1)

            def rank_and_gate(b, place):
                dve.wait_ge(s_rkps, b + 1)
                nc.vector.tensor_tensor_reduce(rank_tmp[:, :], p_rk[0:T, 0:E], hot[:, :], 1.0, 0.0,
                                               ALU.mult, ALU.add, rank[:, :]).then_inc(s_rank, 1)
                nc.vector.tensor_tensor(hot_sum[:, :], hot_sum[:, :], hot[:, :], ALU.add).then_inc(s_sum, 1)
                dve.wait_ge(s_rank, b + 1)
                nc.vector.tensor_scalar(over[:, :], thr[0:T], rank[:, 0:1], None, ALU.is_le).then_inc(s_over, 1)
                dve.wait_ge(s_over, b + 1)
                nc.vector.tensor_reduce(quot[:, :], over[:, :], AX.X, ALU.add).then_inc(s_quot, 1)
                dve.wait_ge(s_quot, b + 1)
                nc.vector.scalar_tensor_tensor(out=rest[:, :], in0=quot[:, :], scalar=-float(BLK), in1=rank[:, :],
                                               op0=ALU.mult, op1=ALU.add).then_inc(s_rest, 1)
                nc.vector.tensor_scalar(quot_all[:, bass.ds(b, 1)], quot[:, :], 1.0, None, ALU.mult)
                dve.wait_ge(s_rest, b + 1)
                here = row_hot[:, bass.ds(b, 1), :].rearrange("p o n -> p (o n)")
                nc.vector.tensor_scalar(here, rows64, rest[:, 0:1], None, ALU.is_equal).then_inc(s_rowhot, 1)
                dve.wait_ge(s_tanh, b + 1)
                nc.vector.tensor_scalar(xw[:, place, 0, HD:XW], gate[:, :], 0.5, 0.5, ALU.mult, ALU.add)
                nc.vector.tensor_scalar(xw[:, place, 1, HD:XW], gate[:, :], 0.5, 0.5, ALU.mult, ALU.add
                                        ).then_inc(s_gate, 1)

            def hidden(b, part):
                lo, hi = ((0, SA), (SA, S))[part]
                dve.wait_ge(s_gelu[part], b + 1)
                nc.vector.tensor_tensor(hid[:, lo:hi], hid[:, lo:hi], (p_xa, p_xb)[part][0:T, 0:hi - lo], ALU.mult
                                        ).then_inc(s_hid[part], 1)

            def step(b, rnd, place, first, last_batch):
                hidden(b, 0)
                hidden(b, 1)
                if not last_batch:
                    dve.wait_ge(s_xnps, b + 1)
                    norm_x(b + 1, rnd + (place + 1) // RING, (place + 1) % RING)
                if not first:
                    route(b - 1)
                    rank_and_gate(b - 1, (place - 1) % RING)
                dve.wait_ge(s_att, b + 1)
                dve.wait_ge(s_xwrow[place], 16 * rnd + 16)
                x2 = xw[:, place, :, 0:HD]
                nc.vector.tensor_tensor(x2, xin[:, place, :].rearrange("p (h d) -> p h d", h=2),
                                        p_att[0:T, :].rearrange("p (h d) -> p h d", h=2), ALU.add).then_inc(s_x2, 1)
                dve.wait_ge(s_x2, b + 1)
                dve.wait_ge(s_trow, 16 * b + 16)
                norm(b, x2, bn_t, ag_t, ve_t, rs_t, s_bnt, s_agt, s_vet, s_rst,
                     tn[:, :].rearrange("p (h d) -> p h d", h=2), s_t)

            nc.vector.memset(hot_sum[:, :], 0.0).then_inc(s_sum, 1)
            norm_x(0, 0, 0)
            dve.wait_ge(s_con, 48)
            batches(dve, step)
            route(NB - 1)
            rank_and_gate(NB - 1, (NB - 1) % RING)

            dve.wait_ge(s_cntps, 1)
            nc.vector.tensor_tensor(cnt_over, p_lg[:, 0:E].unsqueeze(2).to_broadcast([P, E, NTHR]),
                                    thr.unsqueeze(1).to_broadcast([P, E, NTHR]), ALU.is_gt).then_inc(s_table2, 1)
            dve.wait_ge(s_table2, 1)
            nc.vector.tensor_reduce(extra[:, :], cnt_over, AX.X, ALU.add).then_inc(s_table2, 1)
            dve.wait_ge(s_table2, 2)
            nc.vector.tensor_tensor(before_of, extra[:, :].unsqueeze(1).to_broadcast([P, E, E]), e_before, ALU.mult
                                    ).then_inc(s_table2, 1)
            dve.wait_ge(s_table2, 3)
            nc.vector.tensor_reduce(start[:, :], before_of, AX.X, ALU.add).then_inc(s_table2, 1)
            dve.wait_ge(s_table2, 4)
            nc.vector.tensor_tensor(start[:, :], start[:, :], e_num, ALU.add).then_inc(s_table2, 1)
            dve.wait_ge(s_table2, 5)
            dve.wait_ge(s_rowhot, 2 * NB)
            nc.vector.tensor_tensor(start_tok, hot_all[:, :, :], start[0:T, :].unsqueeze(1).to_broadcast([T, NB, E]),
                                    ALU.mult).then_inc(s_table2, 1)
            nc.vector.scalar_tensor_tensor(out=ends[:, 0:E], in0=start[:, :], scalar=1.0, in1=extra[:, :],
                                           op0=ALU.add, op1=ALU.add)
            nc.vector.tensor_tensor(ends[:, E:E + 1], start[:, E - 1:E], extra[:, E - 1:E], ALU.add
                                    ).then_inc(s_table, 1)
            dve.wait_ge(s_table2, 6)
            nc.vector.tensor_reduce(blk_of[:, :], start_tok, AX.X, ALU.add).then_inc(s_table2, 1)
            dve.wait_ge(s_table2, 7)
            nc.vector.tensor_tensor(blk_of[:, :], blk_of[:, :], quot_all[:, :], ALU.add).then_inc(s_table2, 1)
            dve.wait_ge(s_table2, 8)
            nc.vector.tensor_tensor(blk_hot, blks.unsqueeze(1).to_broadcast([T, NB, NCOL]),
                                    blk_of[:, :].unsqueeze(2).to_broadcast([T, NB, NCOL]), ALU.is_equal
                                    ).then_inc(s_table2, 1)
            dve.wait_ge(s_table2, 9)
            nc.vector.tensor_tensor(blk_hot, blk_hot, tok_low.unsqueeze(2).to_broadcast([T, NB, NCOL]), ALU.mult
                                    ).then_inc(s_blkhot, 1)
            dve.wait_ge(s_idps, 1)
            for h in range(2):
                half = slice(BLK * h, BLK * h + BLK)
                nc.vector.tensor_scalar(id_tok[half, 0:NCOL - 1], p_rk[half, h:NCOL - 1 + h], float(TOK), None, ALU.add
                                        ).then_inc(s_ids, 1)
            nc.vector.tensor_scalar(id_half[:, :], p_rk[:, 0:NCOL], 2.0, halves, ALU.mult, ALU.add).then_inc(s_ids, 1)

            def finish(j):
                odd = dve.snap(j % 2) if not isinstance(j, int) else j % 2
                xg = g_x2[:, bass.ds(odd * XW, HD)]
                gates = g_x2[:, bass.ds(odd * XW + HD, 1)]
                yo = y_out2[:, bass.ds(odd * HD, HD)]
                dve.wait_ge(s_gx, 16 * j + 16)
                dve.wait_ge(s_y_free, j + 1)
                dve.wait_ge(s_y, j + 1)
                nc.vector.scalar_tensor_tensor(out=yo, in0=p_y[:, 0:HD], scalar=gates, in1=xg,
                                               op0=ALU.mult, op1=ALU.add).then_inc(s_yo, 1)

            def unit(j, e, rnd, slot, before, first):
                by_size(dve, j, lambda large: unit_of(j, e, rnd, slot, before, first, large))

            def unit_of(j, e, rnd, slot, before, first, large):
                dve.wait_ge(s_hp, j + 1)
                cols = slice(0, D if large else 2 * P)
                nc.vector.tensor_copy(h_pre[:, cols], p_h[:, cols]).then_inc(s_hc, 1)
                n = BLK if large else SMALL
                bias = b1s[:, bass.ds(e, 1), :].rearrange("p o c -> p (o c)").unsqueeze(2).to_broadcast([P, KF, n])
                dve.wait_ge(s_hTp, j + 1)
                nc.vector.tensor_tensor(hT[:, :, 0:n], p_hT[:, 0:KF * n].rearrange("p (c t) -> p c t", c=KF), bias,
                                        ALU.add).then_inc(s_hb, 1)
                if before is not None:
                    finish(j - 1)

            nc.vector.memset(hT[:, :, :], 0.0).then_inc(s_hT0, 1)
            dve.wait_ge(s_hT0, 1)
            dve.sem_inc(s_yo, 1)
            dve.wait_ge(s_table, 1)
            dve.wait_ge(s_ids, 3)
            last = blocks_of_experts(dve, unit)
            finish(last)

        @block.gpsimd
        def _(pool):
            def apart():
                pool.sem_inc(s_apart_p, 1)

            def inverse_root(b, ve, rs, s_ve, s_rs):
                pool.wait_ge(s_ve, b + 1)
                nc.gpsimd.tensor_tensor(rs[:, :], ve[:, :], neg_half, ALU.pow).then_inc(s_rs, 1)

            def step(b, rnd, place, first, last_batch):
                if not last_batch:
                    inverse_root(b + 1, ve_x, rs_x, s_vex, s_rsx)
                inverse_root(b, ve_t, rs_t, s_vet, s_rst)

            pool.sem_inc(s_trow, 16)
            for r in range(RING):
                pool.sem_inc(s_xwrow[r], 16)
            bound_t, bound_x = pool.to_reg(TOK - 1), pool.to_reg(2 * TOK - 1)
            pool.wait_ge(s_con0, 16)
            inverse_root(0, ve_x, rs_x, s_vex, s_rsx)
            batches(pool, step)

            def column(j):
                return slice(j, j + 1) if isinstance(j, int) else bass.ds(j, 1)

            def gather_t(j, buf):
                if isinstance(j, int):
                    at = id_tok[:, column(j)]
                    pool.sem_inc(s_at_t, 2)
                else:
                    at = at_t[buf][:, :]
                    nc.gpsimd.tensor_copy(at, id_tok[:, column(j)]).then_inc(s_at_t, 2)
                    pool.wait_ge(s_at_t, j + 2)
                    apart()
                nc.gpsimd.indirect_dma_start(g_t[buf], None, t_rows, bass.IndirectOffsetOnAxis(ap=at, axis=0),
                                             bounds_check=bound_t, oob_is_err=False).then_inc(s_gt[buf], 16)

            def gather_x(j, par):
                nc.gpsimd.tensor_copy(at_x[par][:, :], id_half[:, column(j)]).then_inc(s_at_x, 1)
                pool.wait_ge(s_at_x, j + 1)
                apart()
                nc.gpsimd.indirect_dma_start(g_x[par], None, xw_rows,
                                             bass.IndirectOffsetOnAxis(ap=at_x[par][:, :], axis=0),
                                             bounds_check=bound_x, oob_is_err=False).then_inc(s_gx, 16)

            def scatter(j, par):
                nc.gpsimd.tensor_copy(at_out[par][:, :], id_half[:, column(j)]).then_inc(s_at_out, 1)
                pool.wait_ge(s_at_out, j + 1)
                pool.wait_ge(s_yo, j + 2)
                apart()
                nc.gpsimd.indirect_dma_start(out_halves, bass.IndirectOffsetOnAxis(ap=at_out[par][:, :], axis=0),
                                             y_out[par], None, bounds_check=bound_x, oob_is_err=False
                                             ).then_inc(s_done[par], 16)

            pool.wait_ge(s_att, NB)
            for g in (*g_t, g_x2):
                nc.gpsimd.memset(g, 0.0).then_inc(s_g0, 1)
            pool.wait_ge(s_trow, 16 * NB + 16)
            pool.wait_ge(s_g0, 3)
            pool.wait_ge(s_ids, 2)
            gather_t(0, 0)
            gather_t(2, 1)
            pool.wait_ge(s_ids, 3)
            for r in range(RING):
                pool.wait_ge(s_xwrow[r], 16 * (1 + len(range(r, NB, RING))))
            gather_x(0, 0)
            last = last_block(pool)

            def fetch_pair(j, buf):
                pool.wait_ge(s_bps, j + 2)
                apart()
                gather_t(j + 4, buf)

            def block_step(j, par):
                if isinstance(j, int):
                    if par == 0:
                        fetch_pair(j, 0)
                    if j > 0:
                        scatter(j - 1, 1 - par)
                else:
                    if par == 0:
                        with pool.If(pool.snap(j % 4) > 1):
                            fetch_pair(j, 1)
                        with pool.Else():
                            fetch_pair(j, 0)
                    scatter(j - 1, 1 - par)
                pool.wait_ge(s_gx, 16 * j + 16)
                apart()
                gather_x(j + 1, 1 - par)
                if not isinstance(j, int):
                    pool.wait_ge(s_done[par], 8 * (j - par))
                pool.sem_inc(s_y_free, 1)

            block_step(0, 0)
            block_step(1, 1)
            with pool.Fori(2, last + 1) as j:
                by_parity(pool, j, lambda par: block_step(j, par))
            by_parity(pool, last, lambda par: scatter(last, par))

            pool.wait_ge(s_gx, 16 * last + 32)
            apart()
            with pool.If(pool.snap(last % 2) > 0):
                pool.wait_ge(s_done[0], 8 * last + 8)
                pool.wait_ge(s_done[1], 8 * last + 8)
                pool.sem_inc(s_apart_p, 1)
                with pool.If(pool.snap(last % 4) > 1):
                    pool.wait_ge(s_gt[0], 4 * last + 20)
                    pool.wait_ge(s_gt[1], 4 * last + 20)
                    pool.sem_inc(s_apart_p, 1)
                with pool.Else():
                    pool.wait_ge(s_gt[0], 4 * last + 28)
                    pool.wait_ge(s_gt[1], 4 * last + 12)
                    pool.sem_inc(s_apart_p, 1)
            with pool.Else():
                pool.wait_ge(s_done[0], 8 * last + 16)
                pool.wait_ge(s_done[1], 8 * last)
                pool.sem_inc(s_apart_p, 1)
                with pool.If(pool.snap(last % 4) > 1):
                    pool.wait_ge(s_gt[0], 4 * last + 24)
                    pool.wait_ge(s_gt[1], 4 * last + 24)
                    pool.sem_inc(s_apart_p, 1)
                with pool.Else():
                    pool.wait_ge(s_gt[0], 4 * last + 32)
                    pool.wait_ge(s_gt[1], 4 * last + 16)
                    pool.sem_inc(s_apart_p, 1)


def kernel(x, ctx_1024, L0_ffn_router_w, L0_ffn_w1, L0_ffn_b1, L0_ffn_w2, L0_ffn_b2):
    import concourse.bacc as bacc
    from concourse.bass_utils import run_bass_kernel_spmd

    def laid(a, shape, order):
        return np.ascontiguousarray(np.transpose(np.reshape(np.asarray(a), shape), order))

    ctx = np.asarray(ctx_1024)
    full = P * (SC - 1)
    arrays = {
        "x": np.ascontiguousarray(x),
        "ctx_main": laid(ctx[:, 0:full], (NB, SC - 1, P, D), (0, 2, 1, 3)),
        "ctx_rest": np.ascontiguousarray(ctx[:, full:S]),
        "ctxT_a": laid(ctx[:, 0:SA], (NB, SA, KD, P), (0, 3, 2, 1)),
        "ctxT_b": laid(ctx[:, SA:S], (NB, S - SA, KD, P), (0, 3, 2, 1)),
        "router": laid(L0_ffn_router_w, (KD, P, E), (1, 0, 2)),
        "w1": laid(L0_ffn_w1, (E, KD, P, F), (0, 2, 1, 3)),
        "b1": laid(L0_ffn_b1, (E, 2, 4, P), (3, 0, 2, 1)).reshape(P, E, KF),
        "w2": laid(L0_ffn_w2, (E, KF, P, D), (0, 2, 1, 3)),
        "b2": np.ascontiguousarray(L0_ffn_b2),
        "consts": shape_constants(),
    }
    nc = bacc.Bacc("TRN2", target_bir_lowering=False, num_devices=1)
    args = [nc.dram_tensor(f"in_{n}", a.shape, mybir.dt.from_np(a.dtype), kind="ExternalInput").ap()
            for n, a in arrays.items()]
    out = nc.dram_tensor("out", (NB, T, D), F32, kind="ExternalOutput").ap()
    build(nc, *args, out)
    r = run_bass_kernel_spmd(nc, [{f"in_{n}": a for n, a in arrays.items()}], core_ids=[0])
    return r.results[0]["out"]
```
